# Optimizing a Trainium2 kernel written in Bass

```python
import numpy as np
import jax
import jax.numpy as jnp

def _softmax(x, axis=-1):
    return jax.nn.softmax(x, axis=axis)

def _gelu(x):
    return jax.nn.gelu(x, approximate=True)

def _silu(x):
    return jax.nn.silu(x)

def _sigmoid(x):
    return jax.nn.sigmoid(x)

def _layernorm(x, axis=-1, eps=1e-05):
    m = jnp.mean(x, axis=axis, keepdims=True)
    v = jnp.var(x, axis=axis, keepdims=True)
    return (x - m) / jnp.sqrt(v + eps)

def _scatter_add(tgt, idx, src, axis=0):
    return tgt.at[idx].add(src)

def _segment_sum(src, seg, n):
    return jax.ops.segment_sum(src, seg, n)
kernel_name = 'mk_adj_preln_d4_adj_r2_e48ccd'

def setup_inputs(seed: int=0):
    np.random.seed(seed)
    _w = jnp.asarray

    def _rec_inputs():
        import jax
        import jax.numpy as jnp
        _gk = jax.random.key(seed)
        x = -0.0005207 + 1.001 * jax.random.normal(jax.random.fold_in(_gk, 1), (4096, 128), jnp.float32)
        _a = jax.random.bernoulli(jax.random.fold_in(_gk, 2), 0.000976562, (4096, 4096))
        _a = jnp.logical_or(_a, jnp.swapaxes(_a, -1, -2))
        _a = jnp.logical_or(_a, jnp.eye(4096, dtype=bool))
        _af = _a.astype(jnp.float32)
        _af = _af * jax.random.uniform(jax.random.fold_in(_gk, 3), (4096, 4096), jnp.float32, 0.05, 1)
        adj = _af
        return (x, adj)
    x, adj = _rec_inputs()

    def _L0_gnn_setup():
        import jax, jax.numpy as jnp
        import numpy as np
        N = 8192
        IN_DIM = 128
        OUT_DIM = 128

        def _message(X, A, W):
            deg = jnp.sum(A, axis=1, keepdims=True)
            A_norm = A / jnp.where(deg > 0, deg, 1.0)
            return A_norm @ X @ W
        key = jax.random.key(seed)
        k1, k2, k3, k4 = jax.random.split(key, 4)
        X = jax.random.normal(k1, (N, IN_DIM), dtype=jnp.float32)
        A = jax.random.uniform(k2, (N, N), dtype=jnp.float32)
        W_in = jax.random.normal(k3, (IN_DIM, OUT_DIM), dtype=jnp.float32) / np.sqrt(IN_DIM)
        W_out = jax.random.normal(k4, (IN_DIM, OUT_DIM), dtype=jnp.float32) / np.sqrt(IN_DIM)
        return {'X': X, 'A': A, 'W_in': W_in, 'W_out': W_out}
    _L0_gnn_all = _L0_gnn_setup()
    _L0_gnn_in = {k: v for k, v in _L0_gnn_all.items() if k in ('W_in', 'W_out')}
    del _L0_gnn_all

    def _L1_gnn_setup():
        import jax, jax.numpy as jnp
        import numpy as np
        N, E, D = (4096, 4096, 128)
        key = jax.random.key(seed)
        k1, k2 = jax.random.split(key)
        X = jax.random.normal(k1, (N, D), dtype=jnp.float32)
        H = jax.random.uniform(k2, (N, E), dtype=jnp.float32)
        return {'X': X, 'H': H}
    _L1_gnn_all = _L1_gnn_setup()
    _L1_gnn_in = {k: v for k, v in _L1_gnn_all.items() if k in ()}
    del _L1_gnn_all

    def _L2_gnn_setup():
        import jax, jax.numpy as jnp
        import numpy as np
        N = 8192
        F_IN = 128
        F_OUT = 128
        key = jax.random.key(seed)
        k1, k2, k3 = jax.random.split(key, 3)
        x = jax.random.normal(k1, (N, F_IN), dtype=jnp.float32)
        adj = jax.random.uniform(k2, (N, N), dtype=jnp.float32)
        stdv = 1.0 / np.sqrt(F_OUT)
        w = jax.random.uniform(k3, (2 * F_IN, F_OUT), dtype=jnp.float32, minval=-stdv, maxval=stdv)
        return {'input': x, 'adj': adj, 'weight': w}
    _L2_gnn_all = _L2_gnn_setup()
    _L2_gnn_in = {k: v for k, v in _L2_gnn_all.items() if k in ('weight',)}
    del _L2_gnn_all

    def _L3_gnn_setup():
        import jax, jax.numpy as jnp
        import numpy as np
        N = 8192
        U = 128
        AVG_DEGREE = 32
        key = jax.random.key(seed)
        kx, ka, kw = jax.random.split(key, 3)
        x = jax.random.normal(kx, (N, U), dtype=jnp.float32)
        adj = (jax.random.uniform(ka, (N, N)) < AVG_DEGREE / N).astype(jnp.float32)
        W = jax.random.normal(kw, (U, U), dtype=jnp.float32) * 0.05
        b = jnp.zeros((U,), dtype=jnp.float32)
        return {'x': x, 'adj': adj, 'W': W, 'b': b}
    _L3_gnn_all = _L3_gnn_setup()
    _L3_gnn_in = {k: v for k, v in _L3_gnn_all.items() if k in ('W', 'b')}
    del _L3_gnn_all
    return {'x': x, 'adj': adj, 'L0_gnn_W_in': _L0_gnn_in['W_in'], 'L0_gnn_W_out': _L0_gnn_in['W_out'], 'L2_gnn_weight': _L2_gnn_in['weight'], 'L3_gnn_W': _L3_gnn_in['W'], 'L3_gnn_b': _L3_gnn_in['b']}

def reference(x, adj, L0_gnn_W_in, L0_gnn_W_out, L2_gnn_weight, L3_gnn_W, L3_gnn_b):
    import jax
    import jax.numpy as jnp

    def _L0_gnn_ref(X, A, W_in, W_out):
        import jax, jax.numpy as jnp
        import numpy as np
        N = 8192
        IN_DIM = 128
        OUT_DIM = 128

        def _message(X, A, W):
            deg = jnp.sum(A, axis=1, keepdims=True)
            A_norm = A / jnp.where(deg > 0, deg, 1.0)
            return A_norm @ X @ W
        X_in = _message(X, A, W_in)
        X_out = _message(X, A.T, W_out)
        return X_in + X_out

    def _L1_gnn_ref(X, H):
        import jax, jax.numpy as jnp
        import numpy as np
        N, E, D = (4096, 4096, 128)
        msg = jnp.matmul(H.T, X)
        inv_deg = 1.0 / H.sum(axis=0)
        inv_deg = jnp.where(jnp.isinf(inv_deg), 0.0, inv_deg)
        return msg * inv_deg[:, None]

    def _L2_gnn_ref(input, adj, weight):
        import jax, jax.numpy as jnp
        import numpy as np
        N = 8192
        F_IN = 128
        F_OUT = 128
        support = adj @ input
        h = jnp.concatenate([input, support], axis=1)
        return h @ weight

    def _L3_gnn_ref(x, adj, W, b):
        import jax, jax.numpy as jnp
        import numpy as np
        N = 8192
        U = 128
        AVG_DEGREE = 32
        adj = jax.lax.stop_gradient(adj)
        neigh1 = adj @ x
        x1 = jax.nn.swish(neigh1 @ W + b)
        neigh2 = adj @ x1
        x2 = jax.nn.swish(neigh2 @ W + b)
        return x2
    h = jnp.maximum(_layernorm(x, axis=-1), 0.0)
    x = x + _L0_gnn_ref(h, adj, L0_gnn_W_in, L0_gnn_W_out)
    h = jnp.maximum(_layernorm(x, axis=-1), 0.0)
    x = x + _L1_gnn_ref(h, adj)
    h = jnp.maximum(_layernorm(x, axis=-1), 0.0)
    x = x + _L2_gnn_ref(h, adj, L2_gnn_weight)
    h = jnp.maximum(_layernorm(x, axis=-1), 0.0)
    x = x + _L3_gnn_ref(h, adj, L3_gnn_W, L3_gnn_b)
    return x

_drawn_inputs = setup_inputs


def setup_inputs(seed=0):
    import zlib

    import numpy as np

    out = dict(_drawn_inputs(seed))
    spreads = {'L3_gnn_b': (0.0, 0.1)}
    factors = {}
    for name, (base, spread) in spreads.items():
        noise = np.random.default_rng([zlib.crc32(name.encode()), seed]).standard_normal(out[name].shape)
        drawn = base * np.exp(spread * noise) if base else spread * noise
        out[name] = jnp.asarray(drawn.astype(out[name].dtype))
    for name, factor in factors.items():
        out[name] = (out[name] * factor).astype(out[name].dtype)
    return out
```

```python
from contextlib import ExitStack

import concourse.bass as bass
from concourse import mybir

P = 128
BANK = 512
F32 = mybir.dt.float32
F32R = mybir.dt.float32r
ALU = mybir.AluOpType
ACT = mybir.ActivationFunctionType
AX = mybir.AxisListType
FLT_MAX = 3.4028234663852886e38
EPS = 1e-5


def gnn_stack_kernel(nc, x_in, adj, w_in, w_out, w_l2, w_l3, b_l3, out):
    N, D = x_in.shape
    assert D == P and N == 4096
    T = N // P
    WIDE = 1024
    SL = N // WIDE
    TS = WIDE // P
    GT = BANK // P
    NG = T // GT
    SUP = N // BANK
    SLOTS = SUP * 4
    LAG = 2
    RES = 2
    NRAW = 5
    RING0, RING1, RING2 = 4, 4, 5
    PAIRS1 = T // 2
    PAIRS2 = (T - RES) // 2

    adj_t = adj.rearrange("(t p) c -> p t c", p=P)
    x_t = x_in.rearrange("(t p) d -> p t d", p=P)
    out_t = out.rearrange("(t p) d -> p t d", p=P)
    adjT = nc.dram_tensor("adjT_scratch", [SL, T - RES, P, WIDE], F32, kind="Internal").ap()
    adjT_v = adjT.rearrange("s t p c -> p s t c")

    ctx = ExitStack()
    with ctx:
        def sb(name, shape, dt=F32):
            return ctx.enter_context(nc.sbuf_tensor(name, shape, dt))

        def sem(name):
            return ctx.enter_context(nc.semaphore(name))

        raw = sb("raw", [P, NRAW, 2, WIDE])
        hi = sb("hi", [P, 4, WIDE], F32R)
        lo = sb("lo", [P, 4, WIDE], F32R)
        stage = sb("stage", [P, 4, 2, BANK])
        res = sb("res", [P, RES, N])
        h_hi = sb("h_hi", [P, T * P], F32R)
        h_lo = sb("h_lo", [P, T * P], F32R)
        hj_hi = sb("hj_hi", [P, WIDE], F32R)
        hj_lo = sb("hj_lo", [P, WIDE], F32R)
        acc = sb("acc", [P, N])
        x = sb("x", [P, T * P])
        pt = sb("pt", [P, WIDE])
        wi = sb("wi", [P, P])
        wo = sb("wo", [P, P])
        w2a = sb("w2a", [P, P])
        w2b = sb("w2b", [P, P])
        w3 = sb("w3", [P, P])
        b3 = sb("b3", [P, P])
        ident = sb("ident", [P, P])
        rs_part = sb("rs_part", [P, SL, T])
        cs_part = sb("cs_part", [P, TS, SUP])
        rs = sb("rs", [P, T])
        rs_pos = sb("rs_pos", [P, T])
        rs_den = sb("rs_den", [P, T])
        rs_inv = sb("rs_inv", [P, T])
        cs = sb("cs", [P, T])
        cs_pos = sb("cs_pos", [P, TS])
        cs_is0 = sb("cs_is0", [P, TS])
        cs_den = sb("cs_den", [P, TS])
        cs_inv = sb("cs_inv", [P, TS])
        rs_is0 = sb("rs_is0", [P, T])
        c1_raw = sb("c1_raw", [P, T])
        c1_safe = sb("c1_safe", [P, T])
        c1_ok = sb("c1_ok", [P, T])
        c1 = sb("c1", [P, T])
        stats = sb("stats", [P, 2, GT, 6])
        meanvar = sb("meanvar", [P, 2, GT, 2])
        var_eps = sb("var_eps", [P, 2, GT])
        rstd = sb("rstd", [P, 2, GT])
        minus_half = sb("minus_half", [P, GT])

        psP = ctx.enter_context(nc.psum_tensor("psP", [P, 2, BANK], F32))
        psT = ctx.enter_context(nc.psum_tensor("psT", [P, 2, BANK], F32))
        psQ = ctx.enter_context(nc.psum_tensor("psQ", [P, 2, BANK], F32))
        psE = ctx.enter_context(nc.psum_tensor("psE", [P, 2, BANK], F32))

        raw_in = [sem(f"raw_in{s}") for s in range(NRAW)]
        x_loaded = [sem(f"x_loaded{q}") for q in range(SL)]
        w_in_sem = sem("weights_loaded")
        ident_ok = sem("ident_ok")
        ident_zero = sem("ident_zero")
        nat_hi = sem("nat_hi")
        nat_lo = sem("nat_lo")
        nat_used = sem("nat_used")
        t_done = sem("t_done")
        t_out = sem("t_out")
        t_hi = sem("t_hi")
        t_hi_act = sem("t_hi_act")
        t_lo = sem("t_lo")
        t_used = sem("t_used")
        stored = [sem(f"stored{h}") for h in range(2)]
        acc_zero = sem("acc_zero")
        q_added = sem("q_added")
        hj_ok = sem("hj_ok")
        cs_sum = sem("cs_sum")
        rs_sum = sem("rs_sum")
        cs_step = sem("cs_step")
        cs_den_ok = sem("cs_den_ok")
        cs_inv_ok = sem("cs_inv_ok")
        rs_step = sem("rs_step")
        rs_den_ok = sem("rs_den_ok")
        rs_inv_ok = sem("rs_inv_ok")
        c1_step = sem("c1_step")
        a_hi = sem("a_hi")
        a_lo = sem("a_lo")
        a_used = sem("a_used")
        p_half = sem("p_half")
        p_out = sem("p_out")
        e_done = sem("e_done")
        e_used = sem("e_used")
        ln_stats = sem("ln_stats")
        ln_mv = sem("ln_mv")
        ln_eps = sem("ln_eps")
        ln_rstd = sem("ln_rstd")
        half_ok = sem("half_ok")
        hn_ok = sem("hn_ok")
        pool_late = sem("pool_late")
        hs_hi = sem("hs_hi")
        hs_lo = sem("hs_lo")
        ht_done = sem("ht_done")
        ht_out = sem("ht_out")
        g_done = sem("g_done")
        g_used = sem("g_used")
        y_ok = sem("y_ok")
        o_ok = sem("o_ok")
        o_out = sem("o_out")

        def f32(ap):
            return ap.bitcast(F32)

        def cols(t, first, n):
            return t[:, bass.ds(first, n)]

        def base(p):
            return T * SL * (p - 1)

        def ring(p):
            return RING1 if p == 1 else RING2

        def raw_count(p, oc, kk):
            s = kk % ring(p)
            before = SL * SUP * 2 // RING0 if s < RING0 else 0
            if p >= 2:
                before += (SL * PAIRS1 // RING1 if s < RING1 else 0) + (p - 2) * SL * PAIRS2 // RING2
            uses = (PAIRS1 // RING1) if p == 1 else (PAIRS2 // RING2)
            return (before + oc * uses + kk // ring(p) + 1) * 16

        def tile_src(p, oc, k):
            if p >= 2 and k >= T - RES:
                return res[:, k - (T - RES), bass.ds(oc * WIDE, WIDE)]
            kk = k // 2
            return raw[:, kk % ring(p), k % 2, :]

        def nat_src(q):
            s = q // 4
            return raw[:, (2 * s + (q % 4) // 2) % RING0, q % 2, :]

        def t_dst(J, q):
            if isinstance(J, int) and J == SL - 1 and q % 4 == 3:
                return res[:, :, (q // 4) * BANK:(q // 4 + 1) * BANK]
            return stage[:, q % 4, :, :]

        def hn_view(g):
            return acc[:, g * BANK:(g + 1) * BANK]

        def hi_on_act(q, last):
            return q % 4 != 0 if last else q % 2 == 1

        ACT_HI = SLOTS // 2
        LN0, LN1, LN2, LN3, LN4 = 0, NG, 2 * NG, 3 * NG, 4 * NG
        E0 = 2 * SL + NG

        block = ctx.enter_context(nc.Block())

        @block.sync
        def _(sp):
            def load_super(J, I, guard):
                for half in range(2):
                    s = (2 * I + half) % RING0
                    if guard and half == 0:
                        sp.wait_ge(nat_used, J * SLOTS + I * 4 - 4)
                    sp.dma_start(raw[:, s, :, :],
                                 adj_t[:, 4 * I + 2 * half:4 * I + 2 * half + 2, bass.ds(J * WIDE, WIDE)]
                                 ).then_inc(raw_in[s], 16)

            def store_half(J, I, h):
                n = 2 if (isinstance(J, int) and J == SL - 1 and h == 1) else 4
                sp.wait_ge(t_out, (J * SLOTS + 4 * I + 2 * h + 1) * 2 + (2 if n == 4 else 0))
                src = stage[:, 2 * h:2 * h + n // 2, :, :].rearrange("p u b c -> p (u b) c")
                sp.dma_start(adjT_v[:, I // 2, bass.ds(J * TS + 4 * h, n), (I % 2) * BANK:(I % 2 + 1) * BANK],
                             src).then_inc(stored[h], 16)

            def slab(J, first=False, last=False):
                for I in range(SUP):
                    if I + 1 < SUP:
                        load_super(J, I + 1, guard=not (first and I == 0))
                    elif not last:
                        load_super(J + 1, 0, guard=True)
                    store_half(J, I, 0)
                    store_half(J, I, 1)

            sp.dma_start(x[:, 0:BANK].rearrange("p (t d) -> p t d", d=P), x_t[:, 0:GT, :]).then_inc(x_loaded[0], 16)
            sp.dma_start(x[:, BANK:WIDE].rearrange("p (t d) -> p t d", d=P), x_t[:, GT:TS, :]).then_inc(x_loaded[1], 16)
            load_super(0, 0, guard=False)
            sp.dma_start(x[:, WIDE:2 * WIDE].rearrange("p (t d) -> p t d", d=P), x_t[:, TS:2 * TS, :]).then_inc(x_loaded[2], 16)
            sp.dma_start(x[:, 2 * WIDE:].rearrange("p (t d) -> p t d", d=P), x_t[:, 2 * TS:, :]).then_inc(x_loaded[3], 16)
            for w, src in ((wi, w_in), (wo, w_out), (w2a, w_l2[0:P, :]), (w2b, w_l2[P:2 * P, :]), (w3, w_l3)):
                sp.dma_start(w[:, :], src).then_inc(w_in_sem, 16)
            sp.dma_start(b3[:, :], b_l3.partition_broadcast(P)).then_inc(w_in_sem, 16)
            slab(0, first=True)
            with sp.Fori(1, SL - 1) as J:
                slab(J)
            slab(SL - 1, last=True)

            def load_chunk(p, oc, n_pairs, lead):
                R = ring(p)
                for kk in range(n_pairs):
                    s = kk % R
                    if p == 1 and lead and kk < R:
                        if kk % 2 == 0:
                            sp.wait_ge(nat_used, SL * SLOTS - 4 + 2 * kk)
                    elif kk >= R:
                        sp.wait_ge(a_lo, base(p) + oc * T + 2 * (kk - R) + 2)
                    elif p == 2 and lead:
                        if kk < RING1:
                            sp.wait_ge(a_lo, base(p) - T + 2 * (kk + PAIRS1 - RING1) + 2)
                    else:
                        sp.wait_ge(a_lo, base(p) + oc * T - T + 2 * (kk + n_pairs - R) + 2)
                    if p == 1:
                        src = adj_t[:, 2 * kk:2 * kk + 2, bass.ds(oc * WIDE, WIDE)]
                    else:
                        src = adjT_v[:, bass.ds(oc, 1), 2 * kk:2 * kk + 2, :].rearrange("p s t c -> p (s t) c")
                    sp.dma_start(raw[:, s, :, :], src).then_inc(raw_in[s], 16)

            for p in range(1, 5):
                if p == 2:
                    for h in range(2):
                        sp.wait_ge(stored[h], 16 * SL * SUP)
                n_pairs = PAIRS1 if p == 1 else PAIRS2
                load_chunk(p, 0, n_pairs, True)
                with sp.Fori(1, SL) as oc:
                    load_chunk(p, oc, n_pairs, False)

        @block.gpsimd
        def _(pool):
            pool.memset(ident[:, :], 0.0).then_inc(ident_zero, 1)
            pool.wait_ge(ident_zero, 1)
            pool.affine_select(out=ident[:, :], in_=ident[:, :], compare_op=ALU.not_equal, fill=1.0,
                               base=0, pattern=[[-1, P]], channel_multiplier=1).then_inc(ident_ok, 1)

            pool.memset(minus_half[:, :], -0.5).then_inc(half_ok, 1)
            pool.wait_ge(half_ok, 1)

            def norm_factors(i, index):
                pool.wait_ge(ln_mv, index + 1)
                pool.tensor_scalar(var_eps[:, i, :], meanvar[:, i, :, 1], EPS, None, op0=ALU.add).then_inc(ln_eps, 1)
                pool.wait_ge(ln_eps, index + 1)
                pool.tensor_tensor(rstd[:, i, :], var_eps[:, i, :], minus_half[:, :], ALU.pow).then_inc(ln_rstd, 1)

            def slab(J):
                pool.wait_ge(cs_sum, J + 1)
                pool.tensor_scalar(cs_pos[:, :], cols(cs, J * TS, TS), 0.0, None, op0=ALU.max).then_inc(cs_step, 1)
                pool.tensor_scalar(cs_is0[:, :], cols(cs, J * TS, TS), 0.0, None, op0=ALU.is_le).then_inc(cs_step, 1)
                pool.wait_ge(cs_step, 2 * (J + 1))
                if J > 0:
                    pool.wait_ge(cs_inv_ok, J)
                pool.tensor_tensor(cs_den[:, :], cs_pos[:, :], cs_is0[:, :], ALU.add).then_inc(cs_den_ok, 1)

            for g in range(NG):
                norm_factors(g % 2, LN0 + g)
            slab(0)
            for J in range(1, SL - 1):
                slab(J)
            for I in range(SUP):
                if I >= 2:
                    norm_factors(I % 2, LN1 + I - 2)
                r = slice(GT * I, GT * I + GT)
                pool.wait_ge(rs_sum, I + 1)
                pool.tensor_scalar(rs_pos[:, r], rs[:, r], 0.0, None, op0=ALU.max).then_inc(rs_step, 1)
                pool.tensor_scalar(rs_is0[:, r], rs[:, r], 0.0, None, op0=ALU.is_le).then_inc(rs_step, 1)
                pool.wait_ge(rs_step, 2 * I + 2)
                pool.tensor_tensor(rs_den[:, r], rs_pos[:, r], rs_is0[:, r], ALU.add).then_inc(rs_den_ok, 1)
            slab(SL - 1)
            for g in range(NG - 2, NG):
                norm_factors(g % 2, LN1 + g)
            pool.wait_ge(c1_step, 3)
            pool.tensor_tensor(c1[:, :], c1_safe[:, :], c1_ok[:, :], ALU.mult).then_inc(pool_late, 1)

            def keep_normed(c):
                for i in range(2):
                    n = 2 * (c - 1) + i
                    pool.wait_ge(hn_ok, LN2 + n + 1)
                    pool.tensor_copy(cols(acc, n * BANK, BANK), pt[:, i * BANK:(i + 1) * BANK]).then_inc(pool_late, 1)

            for c in range(1, SL + 1):
                for i in range(2):
                    norm_factors(i, LN2 - 2 + 2 * c + i)
                keep_normed(c)
            for c in range(1, SL + 1):
                for i in range(2):
                    norm_factors(i, LN3 - 2 + 2 * c + i)

        @block.scalar
        def _(act):
            def split_h(g, src, index, func):
                if func == ACT.Copy:
                    act.wait_ge(y_ok, g + 1)
                elif index >= LN2 and index < LN3:
                    act.wait_ge(pool_late, 1 + g + 1)
                else:
                    act.wait_ge(hn_ok, index + 1)
                act.activation(h_hi[:, g * BANK:(g + 1) * BANK], src, func).then_inc(hs_hi, 1)

            def natural_hi(J, q, first):
                g = J * SLOTS + q
                if q % 4 in (0, 2):
                    s = nat_slot(q)
                    act.wait_ge(raw_in[s], raw_super(J, q))
                if not (first and q < 2):
                    act.wait_ge(nat_used, g - 1)
                act.activation(hi[:, q % 2, :], nat_src(q), ACT.Copy,
                               accum_out=rs_part[:, bass.ds(J, 1), q:q + 1].rearrange("p a b -> p (a b)")).then_inc(nat_hi, 1)

            def slab(J, first=False, last=False):
                natural_hi(J, 0, first)
                if not first:
                    for b in range(2):
                        if b == 0:
                            act.wait_ge(p_half, J)
                        else:
                            act.wait_ge(nat_used, J * SLOTS)
                        act.activation(pt[:, b * BANK:(b + 1) * BANK], psP[:, b, :], ACT.Copy).then_inc(p_out, 1)
                    act.wait_ge(cs_sum, J)
                for q in range(SLOTS):
                    g = J * SLOTS + q
                    u = q % 4
                    stays = last and u == 3
                    if q + 1 < SLOTS:
                        natural_hi(J, q + 1, first)
                    if not (first and q < 4) and not stays:
                        act.wait_ge(stored[u // 2], 16 * (J * SUP + q // 4))
                        act.wait_ge(t_lo, g - 3)
                    for b in range(2):
                        act.wait_ge(t_done, 2 * g + b + 1)
                        act.activation(t_dst(J, q)[:, b, :], psT[:, b, :], ACT.Copy,
                                       accum_out=cs_part[:, 2 * u + b, q // 4:q // 4 + 1]).then_inc(t_out, 1)
                    if hi_on_act(q, last):
                        act.wait_ge(t_out, 2 * g + 2)
                        if not (first and q < 2):
                            act.wait_ge(t_used, g - 1)
                        act.activation(hi[:, 2 + q % 2, :].rearrange("p (b c) -> p b c", b=2), t_dst(J, q),
                                       ACT.Copy).then_inc(t_hi_act, 1)
                    if first and q % 4 == 1 and 1 <= q // 4 <= NG - 2:
                        n = q // 4 + 1
                        split_h(n, pt[:, n % 2 * BANK:(n % 2 + 1) * BANK], LN0 + n, ACT.Relu)

            def nat_slot(q):
                return (2 * (q // 4) + (q % 4) // 2) % RING0

            def raw_super(J, q):
                return (J * SUP // 2 + q // 8 + 1) * 16 if isinstance(J, int) else J * (SUP // 2 * 16) + (q // 8 + 1) * 16

            for g in range(2):
                split_h(g, pt[:, g * BANK:(g + 1) * BANK], LN0 + g, ACT.Relu)
            slab(0, first=True)
            with act.Fori(1, SL - 1) as J:
                slab(J)
            slab(SL - 1, last=True)

            def chunk(p, oc, lead):
                prev = p - 1 if lead else p
                for k in range(T):
                    n = base(p) + oc * T + k
                    if not (p >= 2 and k >= T - RES) and k % 2 == 0:
                        act.wait_ge(raw_in[(k // 2) % ring(p)], raw_count(p, oc, k // 2))
                    if p == 1 and lead and k < 4:
                        if k == 0:
                            act.wait_ge(nat_used, SL * SLOTS)
                        if k == 2:
                            act.wait_ge(t_used, SL * SLOTS)
                    else:
                        act.wait_ge(a_used, n - 3)
                    act.activation(hi[:, k % 4, :], tile_src(p, oc, k), ACT.Copy).then_inc(a_hi, 1)
                    if k == 2:
                        for b in range(2):
                            if b == 0:
                                act.wait_ge(p_half, SL * p + oc)
                            elif prev == 0:
                                act.wait_ge(nat_used, SL * SLOTS)
                            else:
                                act.wait_ge(a_used, base(p) + oc * T)
                            if b == 0 and prev == 1:
                                act.wait_ge(pool_late, 1 + 2 * (SL - 1) if lead else 2 * oc - 1)
                            act.activation(pt[:, b * BANK:(b + 1) * BANK], psP[:, b, :], ACT.Copy).then_inc(p_out, 1)
                            if lead and b == 0:
                                split_h(0, hn_view(0), LN0 + NG * p, hfunc(p))
                    if lead:
                        if 3 <= k < 3 + NG - 3:
                            split_h(k - 2, hn_view(k - 2), LN0 + NG * p + k - 2, hfunc(p))
                        if k in (18, 21):
                            g = 6 + (k == 21)
                            split_h(g, hn_view(g), LN0 + NG * p + g, hfunc(p))
                    c = SL if lead else oc
                    for i in range(2):
                        e = E0 + 2 * (SL * (prev - 1) + c - 1) + i
                        if prev == 1 and k == 18 + 2 * i:
                            act.wait_ge(ht_done, 2 * (c - 1) + i + 1)
                            act.activation(stage[:, i, 0, :], psT[:, i, :], ACT.Relu).then_inc(ht_out, 1)
                        if prev == 3 and k == 8 + 2 * i:
                            act.wait_ge(e_used, e + 1)
                            act.activation(cols(acc, (c - 1) * WIDE + i * BANK, BANK), stage[:, i, 1, :],
                                           ACT.Silu).then_inc(y_ok, 1)
                        if prev == 4 and k == 8 + 2 * i:
                            act.wait_ge(e_used, e + 1)
                            act.activation(stage[:, 2 + i, 0, :], stage[:, i, 1, :], ACT.Silu).then_inc(y_ok, 1)
                        if prev == 4 and k == 16 + 2 * i:
                            store_rows(2 * (c - 1) + i)
                if p == 1 and lead:
                    for h in range(2):
                        act.wait_ge(stored[h], 16 * SL * SUP)

            def store_rows(o):
                act.wait_ge(o_ok, o + 1)
                act.dma_start(out_t[:, bass.ds(o * GT, GT), :],
                              cols(x, o * BANK, BANK).rearrange("p (t d) -> p t d", d=P)).then_inc(o_out, 16)

            def hfunc(p):
                return ACT.Copy if p == 4 else ACT.Relu

            for p in range(1, 5):
                chunk(p, 0, True)
                with act.Fori(1, SL) as oc:
                    chunk(p, oc, False)
            for b in range(2):
                if b == 0:
                    act.wait_ge(p_half, SL * 5)
                else:
                    act.wait_ge(a_used, base(5))
                act.activation(pt[:, b * BANK:(b + 1) * BANK], psP[:, b, :], ACT.Copy).then_inc(p_out, 1)
            for i in range(2):
                act.wait_ge(e_used, E0 + 2 * (4 * SL - 1) + i + 1)
                act.activation(stage[:, 2 + i, 0, :], stage[:, i, 1, :], ACT.Silu).then_inc(y_ok, 1)
            for i in range(2):
                store_rows(2 * SL - 2 + i)
            act.wait_ge(o_out, 16 * NG)

        @block.vector
        def _(dve):
            def ln_a(i, rows):
                for t in range(GT):
                    ins = dve.bn_stats(stats[:, i, t, :], rows(t))
                ins.then_inc(ln_stats, 1)

            def ln_b(i):
                for t in range(GT):
                    ins = dve.bn_aggr(meanvar[:, i, t, :], stats[:, i, t, :])
                ins.then_inc(ln_mv, 1)

            def ln_d(i, index, rows, dst):
                dve.wait_ge(ln_rstd, index + 1)
                for t in range(GT):
                    ins = dve.tensor_scalar(dst(t), rows(t), meanvar[:, i, t, 0:1], rstd[:, i, t:t + 1],
                                            op0=ALU.subtract, op1=ALU.mult)
                ins.then_inc(hn_ok, 1)

            def split_h(g, src, index, relu):
                dve.wait_ge(hs_hi, index + 1)
                gs = slice(g * BANK, (g + 1) * BANK)
                if relu:
                    dve.scalar_tensor_tensor(h_lo[:, gs], src, 0.0, f32(h_hi[:, gs]), op0=ALU.max, op1=ALU.subtract).then_inc(hs_lo, 1)
                else:
                    dve.tensor_tensor(h_lo[:, gs], src, f32(h_hi[:, gs]), ALU.subtract).then_inc(hs_lo, 1)

            def x_rows(first_col):
                return lambda t: cols(x, first_col + t * P, P) if not isinstance(first_col, int) \
                    else x[:, first_col + t * P:first_col + (t + 1) * P]

            def acc_rows(first_col):
                return lambda t: cols(acc, first_col + t * P, P) if not isinstance(first_col, int) \
                    else acc[:, first_col + t * P:first_col + (t + 1) * P]

            def scaled_add(e, bank, first_col, inv):
                dve.wait_ge(e_done, e + 1)
                xr = x_rows(first_col)
                for t in range(GT):
                    ins = dve.scalar_tensor_tensor(xr(t), psE[:, bank, t * P:(t + 1) * P], inv(t), xr(t),
                                                   op0=ALU.mult, op1=ALU.add)
                ins.then_inc(e_used, 1)

            def first_rows(g):
                return x_rows(g * BANK)

            def first_hn(g):
                return lambda t: pt[:, (g % 2) * BANK + t * P:(g % 2) * BANK + (t + 1) * P]

            def first_step(g, step):
                i = g % 2
                if step == 0:
                    dve.wait_ge(x_loaded[min(g, 2) if g < 4 else 3], 16)
                    ln_a(i, first_rows(g))
                if step == 1:
                    dve.wait_ge(ln_stats, g + 1)
                    ln_b(i)
                if step == 3:
                    if g >= 2:
                        dve.wait_ge(hs_lo, g - 1)
                    ln_d(i, g, first_rows(g), first_hn(g))

            def natural_lo(J, q):
                g = J * SLOTS + q
                dve.wait_ge(nat_hi, g + 1)
                dve.tensor_tensor(lo[:, q % 2, :], nat_src(q), f32(hi[:, q % 2, :]), ALU.subtract).then_inc(nat_lo, 1)

            def add_q(J, I, first):
                dve.wait_ge(t_used, J * SLOTS + 4 * I + 4)
                a = acc[:, I * BANK:(I + 1) * BANK]
                if first and I < SUP - 1:
                    dve.tensor_copy(a, psQ[:, I % 2, :]).then_inc(q_added, 1)
                else:
                    if I == SUP - 1:
                        dve.wait_ge(acc_zero, 1)
                    dve.wait_ge(q_added, J * SUP + I + 1 - SUP if I < SUP - 1 else J * SUP + I)
                    dve.tensor_tensor(a, psQ[:, I % 2, :], a, ALU.add).then_inc(q_added, 1)

            def slab(J, first=False, last=False):
                if not first and not last:
                    dve.wait_ge(t_used, J * SLOTS)
                    dve.tensor_copy(hj_hi[:, :], f32(cols(h_hi, J * WIDE, WIDE)))
                    dve.tensor_copy(hj_lo[:, :], f32(cols(h_lo, J * WIDE, WIDE))).then_inc(hj_ok, 1)
                natural_lo(J, 0)
                for q in range(SLOTS):
                    g = J * SLOTS + q
                    I, u = q // 4, q % 4
                    ring_t = 2 + q % 2
                    if q + 1 < SLOTS:
                        natural_lo(J, q + 1)
                    by_act = hi_on_act(q, last)
                    if not by_act:
                        dve.wait_ge(t_out, 2 * g + 2)
                        if not (first and q < 2):
                            dve.wait_ge(t_used, g - 1)
                    hi_t = hi[:, ring_t, :].rearrange("p (b c) -> p b c", b=2)
                    lo_t = lo[:, ring_t, :].rearrange("p (b c) -> p b c", b=2)
                    if not by_act:
                        dve.tensor_copy(hi_t, t_dst(J, q)).then_inc(t_hi, 1)
                    if u == 2 and I >= 1:
                        add_q(J, I - 1, first)
                    if first and I + 2 < NG:
                        first_step(I + 2, u)
                    if first and u == 2 and 1 <= I <= NG - 2:
                        n = I + 1
                        split_h(n, pt[:, n % 2 * BANK:(n % 2 + 1) * BANK], LN0 + n, True)
                    if not first:
                        if q == 1:
                            add_q(J - 1, SUP - 1, False)
                            dve.wait_ge(cs_den_ok, J)
                            dve.reciprocal(cs_inv[:, :], cs_den[:, :]).then_inc(cs_inv_ok, 1)
                        if q in (4, 5):
                            i = q - 4
                            if i == 0:
                                dve.wait_ge(cs_inv_ok, J)
                            scaled_add(2 * (J - 1) + i, i, J * WIDE - WIDE + i * BANK,
                                       lambda t, i=i: cs_inv[:, i * GT + t:i * GT + t + 1])
                    n_act = J * ACT_HI + sum(hi_on_act(r, last) for r in range(q + 1))
                    n_dve = J * (SLOTS - ACT_HI) + sum(not hi_on_act(r, last) for r in range(q + 1))
                    if by_act:
                        dve.wait_ge(t_hi_act, n_act)
                    else:
                        dve.wait_ge(t_hi, n_dve)
                    dve.tensor_tensor(lo_t, t_dst(J, q), f32(hi_t), ALU.subtract).then_inc(t_lo, 1)
                    if last:
                        if u == 0 and I >= 3:
                            ln_group(I - 3, 3)
                        if u == 0 and I >= 2:
                            row_update(I - 2)
                        if u >= 1 and I >= 2:
                            ln_group(I - 2, u - 1)
                        if u == 2 and I >= 1:
                            row_factors(I - 1)
                        if u == 3:
                            dve.wait_ge(nat_hi, J * SLOTS + q + 1)
                            part = rs_part[:, :, GT * I:GT * I + GT].rearrange("p s t -> p t s")
                            dve.reduce_sum(rs[:, GT * I:GT * I + GT], part, axis=AX.X).then_inc(rs_sum, 1)
                dve.wait_ge(t_out, J * SLOTS * 2 + SLOTS * 2)
                dve.reduce_sum(cols(cs, J * TS, TS), cs_part[:, :, :], axis=AX.X).then_inc(cs_sum, 1)
                if last:
                    ln_group(NG - 3, 3)

            def row_factors(G):
                dve.wait_ge(rs_den_ok, G + 1)
                r = slice(G * GT, (G + 1) * GT)
                dve.reciprocal(rs_inv[:, r], rs_den[:, r]).then_inc(rs_inv_ok, 1)

            def row_update(G):
                dve.wait_ge(rs_inv_ok, G + 1)
                scaled_add(2 * (SL - 1) + G, G % 2, G * BANK,
                           lambda t: rs_inv[:, G * GT + t:G * GT + t + 1])

            def ln_group(G, step):
                if step == 0:
                    dve.wait_ge(e_used, 2 * (SL - 1) + G + 1)
                    ln_a(G % 2, x_rows(G * BANK))
                if step == 1:
                    dve.wait_ge(ln_stats, LN1 + G + 1)
                    ln_b(G % 2)
                if step == 3:
                    ln_d(G % 2, LN1 + G, x_rows(G * BANK), acc_rows(G * BANK))

            dve.memset(acc[:, N - BANK:], 0.0).then_inc(acc_zero, 1)
            for g in range(2):
                for step in range(4):
                    first_step(g, step)
                split_h(g, pt[:, g * BANK:(g + 1) * BANK], LN0 + g, True)
            slab(0, first=True)
            with dve.Fori(1, SL - 1) as J:
                slab(J)
            slab(SL - 1, last=True)

            def finish(prev, oc, lead, k):
                c = SL if lead else oc
                first_col = c * WIDE - WIDE
                for i in range(2):
                    col = first_col + i * BANK
                    if prev == 0:
                        e = 2 * SL + NG - 2 + i
                        ln = LN1 + NG - 2 + i
                    else:
                        e = E0 + 2 * ((prev - 1) * SL + c - 1) + i
                        ln = LN0 + NG * (prev + 1) + 2 * (c - 1) + i
                    if k == 6 + i:
                        if prev == 0:
                            scaled_add(e, i, col, lambda t: cs_inv[:, i * GT + t:i * GT + t + 1])
                        if prev == 1:
                            if i == 0:
                                dve.wait_ge(pool_late, 1)
                            scaled_add(e, i, col, lambda t: cols(c1, (c - 1) * TS + i * GT + t, 1))
                        if prev == 2:
                            dve.wait_ge(g_used, 2 * (c - 1) + i + 1)
                            dve.wait_ge(e_done, e + 1)
                            dve.tensor_tensor(cols(x, col, BANK), psE[:, i, :], cols(x, col, BANK), ALU.add).then_inc(e_used, 1)
                        if prev >= 3:
                            dve.wait_ge(e_done, e + 1)
                            z = stage[:, i, 1, :].rearrange("p (t d) -> p t d", d=P)
                            row = psE[:, i, :].rearrange("p (t d) -> p t d", d=P)
                            dve.tensor_tensor(z, row, b3[:, :].unsqueeze(1).broadcast_to([P, GT, P]), ALU.add).then_inc(e_used, 1)
                    if prev <= 2:
                        if k == 8 + i:
                            ln_a(i, x_rows(col))
                        if k == 10 + i:
                            ln_b(i)
                        if k == 14 + i:
                            ln_d(i, ln, x_rows(col), acc_rows(col) if prev != 1
                                 else (lambda t: pt[:, i * BANK + t * P:i * BANK + (t + 1) * P]))
                    if prev == 1 and k == 22 + 2 * i:
                        dve.wait_ge(g_done, 2 * (c - 1) + i + 1)
                        dve.tensor_tensor(cols(x, col, BANK), psQ[:, i, :], cols(x, col, BANK), ALU.add).then_inc(g_used, 1)
                    if prev == 4 and k == 12 + 2 * i:
                        o = 2 * (c - 1) + i
                        dve.wait_ge(y_ok, NG + o + 1)
                        dve.tensor_tensor(cols(x, col, BANK), stage[:, 2 + i, 0, :], cols(x, col, BANK), ALU.add).then_inc(o_ok, 1)

            def norm_waits(prev, c, k):
                for i in range(2):
                    e = 2 * SL + NG - 2 + i if prev == 0 else E0 + 2 * ((prev - 1) * SL + c - 1) + i
                    ln = LN1 + NG - 2 + i if prev == 0 else NG * (prev + 1) + 2 * (c - 1) + i
                    if prev <= 2 and k == 8 + i:
                        dve.wait_ge(e_used, e + 1)
                    if prev <= 2 and k == 10 + i:
                        dve.wait_ge(ln_stats, ln + 1)

            def chunk(p, oc, lead):
                prev = p - 1 if lead else p
                for k in range(T):
                    n = base(p) + oc * T + k
                    norm_waits(prev, SL if lead else oc, k)
                    dve.wait_ge(a_hi, n + 1)
                    dve.tensor_tensor(lo[:, k % 4, :], tile_src(p, oc, k), f32(hi[:, k % 4, :]), ALU.subtract).then_inc(a_lo, 1)
                    if p == 1 and lead:
                        if k == 0:
                            add_q(SL - 1, SUP - 1, False)
                            row_factors(NG - 1)
                        if k == 4:
                            dve.wait_ge(cs_den_ok, SL)
                            dve.reciprocal(cs_inv[:, :], cs_den[:, :]).then_inc(cs_inv_ok, 1)
                            dve.wait_ge(cs_sum, SL)
                            dve.reciprocal(c1_raw[:, :], cs[:, :]).then_inc(c1_step, 1)
                        if k == 10:
                            dve.wait_ge(c1_step, 1)
                            dve.tensor_scalar(c1_safe[:, :], c1_raw[:, :], FLT_MAX, -FLT_MAX, op0=ALU.min, op1=ALU.max).then_inc(c1_step, 1)
                        if k == 11:
                            dve.wait_ge(c1_step, 2)
                            dve.tensor_tensor(c1_ok[:, :], c1_safe[:, :], c1_raw[:, :], ALU.is_equal).then_inc(c1_step, 1)
                        if k == 5:
                            row_update(NG - 2)
                            row_update(NG - 1)
                        if k == 6:
                            dve.wait_ge(cs_inv_ok, SL)
                            dve.wait_ge(e_used, 2 * (SL - 1) + NG)
                    if lead:
                        if k == 2:
                            split_h(0, hn_view(0), LN0 + NG * p, p != 4)
                        if 3 <= k < 3 + NG - 3:
                            split_h(k - 2, hn_view(k - 2), LN0 + NG * p + k - 2, p != 4)
                        if k in (18, 21):
                            g = 6 + (k == 21)
                            split_h(g, hn_view(g), LN0 + NG * p + g, p != 4)
                    finish(prev, oc, lead, k)

            for p in range(1, 5):
                chunk(p, 0, True)
                with dve.Fori(1, SL) as oc:
                    chunk(p, oc, False)
            for k in range(16):
                finish(4, None, True, k)

        @block.tensor
        def _(pe):
            def product(dst, w_hi, w_lo, m_hi, m_lo, first, last):
                pe.matmul(dst, w_hi, m_hi, start=first, stop=False)
                pe.matmul(dst, w_hi, m_lo, start=False, stop=False)
                return pe.matmul(dst, w_lo, m_hi, start=False, stop=last)

            def tile_product(k, r, first, last, chunks):
                wh, wl = h_hi[:, k * P:(k + 1) * P], h_lo[:, k * P:(k + 1) * P]
                half = [slice(b * BANK, (b + 1) * BANK) for b in range(2)]
                if first or last:
                    for b in range(2):
                        if first and chunks is not None:
                            pe.wait_ge(p_out, 2 * chunks - 1 + b)
                        end = product(psP[:, b, :], wh, wl, hi[:, r, half[b]], lo[:, r, half[b]], first, last)
                        if last and b == 0:
                            end.then_inc(p_half, 1)
                    return end
                for m in (hi, lo):
                    for b in range(2):
                        pe.matmul(psP[:, b, :], wh, m[:, r, half[b]], start=False, stop=False)
                for b in range(2):
                    end = pe.matmul(psP[:, b, :], wl, hi[:, r, half[b]], start=False, stop=False)
                return end

            def rows(i, t):
                return pt[:, i * BANK + t * P:i * BANK + (t + 1) * P]

            def row_product(e, bank, src, w):
                for t in range(GT):
                    end = pe.matmul(psE[:, bank, t * P:(t + 1) * P], src(t), w[:, :], start=True, stop=True)
                end.then_inc(e_done, 1)

            pe.wait_ge(ident_ok, 1)

            def q_product(J, q, hj):
                I, u = q // 4, q % 4
                g = J * SLOTS + q
                pe.wait_ge(t_lo, g + 1)
                if u == 0 and not (isinstance(J, int) and J == 0 and I < 2):
                    pe.wait_ge(q_added, J * SUP + I - 1)
                for b in range(2):
                    j = 2 * u + b
                    wh, wl = hj(j)
                    bs = slice(b * BANK, (b + 1) * BANK)
                    end = product(psQ[:, I % 2, :], wh, wl, hi[:, 2 + q % 2, bs], lo[:, 2 + q % 2, bs],
                                  first=(j == 0), last=(j == TS - 1))
                end.then_inc(t_used, 1)

            def slab(J, first=False, last=False):
                if first or last:
                    hj = lambda j: (h_hi[:, (J * TS + j) * P:(J * TS + j + 1) * P], h_lo[:, (J * TS + j) * P:(J * TS + j + 1) * P])
                else:
                    hj = lambda j: (hj_hi[:, j * P:(j + 1) * P], hj_lo[:, j * P:(j + 1) * P])
                for q in range(SLOTS + LAG):
                    g = J * SLOTS + q
                    I, u = q // 4, q % 4
                    if q < SLOTS:
                        if u == 0:
                            for half in range(2):
                                s = (2 * I + half) % RING0
                                v = (J * (SUP // 2) + I // 2 + 1) * 16
                                pe.wait_ge(raw_in[s], v)
                        for b in range(2):
                            if not (first and q == 0):
                                pe.wait_ge(t_out, 2 * g + b - 1)
                            j = 2 * u + b
                            for r in range(4):
                                src = raw[:, (2 * I + r // 2) % RING0, r % 2, j * P:(j + 1) * P]
                                end = pe.transpose(psT[:, b, r * P:(r + 1) * P], src, ident[:, :])
                            end.then_inc(t_done, 1)
                        if first and u == 0:
                            pe.wait_ge(hs_lo, max(I + 1, 2))
                        pe.wait_ge(nat_lo, g + 1)
                        tile_product(q, q % 2, q == 0, q == SLOTS - 1,
                                     None if first else J).then_inc(nat_used, 1)
                    if q >= LAG:
                        if q == LAG and not first and not last:
                            pe.wait_ge(hj_ok, J)
                        q_product(J, q - LAG, hj)
                    if not first and q in (2, 3):
                        i = q - 2
                        pe.wait_ge(p_out, 2 * J - 1 + i)
                        row_product(2 * (J - 1) + i, i, lambda t, i=i: rows(i, t), wo)
                    if last and u == 3 and 1 <= I < SUP:
                        G = I - 1
                        e = 2 * (SL - 1) + G
                        pe.wait_ge(q_added, J * SUP + G + 1)
                        pe.wait_ge(e_used, e - 1)
                        row_product(e, G % 2, lambda t, G=G: acc[:, G * BANK + t * P:G * BANK + (t + 1) * P], wi)

            slab(0, first=True)
            pe.wait_ge(w_in_sem, 16 * 6)
            with pe.Fori(1, SL - 1) as J:
                slab(J)
            slab(SL - 1, last=True)

            def finish(prev, c, C, k):
                for i in range(2):
                    col = (c - 1) * WIDE + i * BANK
                    if prev == 0:
                        e = 2 * SL + NG - 2 + i
                    else:
                        e = E0 + 2 * (SL * (prev - 1) + c - 1) + i
                    if prev == 0 and k == 2 and i == 0:
                        G = NG - 1
                        pe.wait_ge(q_added, SL * SUP)
                        pe.wait_ge(e_used, e - 2)
                        row_product(e - 1, G % 2, lambda t: acc[:, G * BANK + t * P:G * BANK + (t + 1) * P], wi)
                    if k == 4 + i:
                        pe.wait_ge(p_out, 2 * C - 1 + i)
                        pe.wait_ge(e_used, e - 1)
                        if prev == 0:
                            row_product(e, i, lambda t: rows(i, t), wo)
                        elif prev == 1:
                            for t in range(GT):
                                end = pe.transpose(psE[:, i, t * P:(t + 1) * P], rows(i, t), ident[:, :])
                            end.then_inc(e_done, 1)
                        else:
                            row_product(e, i, lambda t: rows(i, t), w2b if prev == 2 else w3)
                    if prev == 1 and k == 16 + 2 * i:
                        pe.wait_ge(hn_ok, LN2 + 2 * (c - 1) + i + 1)
                        for t in range(GT):
                            end = pe.transpose(psT[:, i, t * P:(t + 1) * P], rows(i, t), ident[:, :])
                        end.then_inc(ht_done, 1)
                    if prev == 1 and k == 20 + 2 * i:
                        pe.wait_ge(ht_out, 2 * (c - 1) + i + 1)
                        for t in range(GT):
                            end = pe.matmul(psQ[:, i, t * P:(t + 1) * P], stage[:, i, 0, t * P:(t + 1) * P], w2a[:, :],
                                            start=True, stop=True)
                        end.then_inc(g_done, 1)

            def chunk(p, oc, lead):
                C = SL * p + oc
                for k in range(T):
                    n = base(p) + oc * T + k
                    if lead and k % GT == 0:
                        pe.wait_ge(hs_lo, NG * p + k // GT + 1)
                    pe.wait_ge(a_lo, n + 1)
                    tile_product(k, k % 4, k == 0, k == T - 1, C).then_inc(a_used, 1)
                    finish(p - 1 if lead else p, SL if lead else oc, C, k)

            for p in range(1, 5):
                chunk(p, 0, True)
                with pe.Fori(1, SL) as oc:
                    chunk(p, oc, False)
            for k in range(6):
                finish(4, SL, 5 * SL, k)



_OUTS = [((4096, 128), "float32")]
_INS = ["x", "adj", "L0_gnn_W_in", "L0_gnn_W_out", "L2_gnn_weight", "L3_gnn_W", "L3_gnn_b"]


def kernel(**inputs):
    import numpy as _np
    import concourse.bacc as _bacc
    from concourse import mybir as _mybir
    from concourse.bass_utils import run_bass_kernel_spmd as _run

    nc = _bacc.Bacc("TRN2", target_bir_lowering=False, num_devices=1)
    arrays, args = {}, []
    for name in _INS:
        a = _np.ascontiguousarray(inputs[name])
        arrays[f"in_{name}_dram"] = a
        args.append(nc.dram_tensor(f"in_{name}_dram", a.shape, _mybir.dt.from_np(a.dtype), kind="ExternalInput").ap())
    for i, (shape, dtype) in enumerate(_OUTS):
        dt = _mybir.dt.from_np(_np.dtype(dtype))
        args.append(nc.dram_tensor(f"out_{i}_dram", shape, dt, kind="ExternalOutput").ap())
    gnn_stack_kernel(nc, *args)
    r = _run(nc, [arrays], core_ids=[0])
    return r.results[0]["out_0_dram"]
```

```python
from contextlib import ExitStack

import concourse.bass as bass
from concourse import mybir

P = 128
BANK = 512
F32 = mybir.dt.float32
F32R = mybir.dt.float32r
ALU = mybir.AluOpType
ACT = mybir.ActivationFunctionType
AX = mybir.AxisListType
FLT_MAX = 3.4028234663852886e38
EPS = 1e-5


def gnn_stack_kernel(nc, x_in, adj, w_in, w_out, w_l2, w_l3, b_l3, out):
    N, D = x_in.shape
    assert D == P and N == 4096
    T = N // P
    WIDE = 1024
    SL = N // WIDE
    TS = WIDE // P
    GT = BANK // P
    NG = T // GT
    SUP = N // BANK
    SLOTS = SUP * 4
    LAG = 2
    NRAW = 5
    RING0 = 4
    KEEP = 2
    PAIRS = (T - KEEP) // 2

    adj_t = adj.rearrange("(t p) c -> p t c", p=P)
    x_t = x_in.rearrange("(t p) d -> p t d", p=P)
    out_t = out.rearrange("(t p) d -> p t d", p=P)
    adjT = nc.dram_tensor("adjT_scratch", [SL, T, P, WIDE], F32, kind="Internal").ap()
    adjT_v = adjT.rearrange("s t p c -> p s t c")

    ctx = ExitStack()
    with ctx:
        def sb(name, shape, dt=F32):
            return ctx.enter_context(nc.sbuf_tensor(name, shape, dt))

        def sem(name):
            return ctx.enter_context(nc.semaphore(name))

        raw = sb("raw", [P, NRAW, 2, WIDE])
        hi = sb("hi", [P, 4, WIDE], F32R)
        lo = sb("lo", [P, 4, WIDE], F32R)
        stage = sb("stage", [P, 4, 2, BANK])
        h_hi = sb("h_hi", [P, T * P], F32R)
        h_lo = sb("h_lo", [P, T * P], F32R)
        KEEP_AT = nc.sbuf_base
        g_hi = sb("g_hi", [P, T * P], F32R)
        g_lo = sb("g_lo", [P, T * P], F32R)
        hj_hi = sb("hj_hi", [P, WIDE], F32R)
        hj_lo = sb("hj_lo", [P, WIDE], F32R)
        keep = nc.alloc_sbuf_tensor_at("keep", [P, KEEP, N], F32, offset=KEEP_AT)
        acc = sb("acc", [P, N])
        x = sb("x", [P, T * P])
        pt = sb("pt", [P, WIDE])
        wi = sb("wi", [P, P])
        wo = sb("wo", [P, P])
        w2a = sb("w2a", [P, P])
        w2b = sb("w2b", [P, P])
        w3 = sb("w3", [P, P])
        b3 = sb("b3", [P, P])
        ident = sb("ident", [P, P])
        rs_part = sb("rs_part", [P, SL, T])
        cs_part = sb("cs_part", [P, TS, SUP])
        rs = sb("rs", [P, T])
        rs_pos = sb("rs_pos", [P, T])
        rs_den = sb("rs_den", [P, T])
        rs_inv = sb("rs_inv", [P, T])
        cs = sb("cs", [P, T])
        cs_pos = sb("cs_pos", [P, TS])
        cs_is0 = sb("cs_is0", [P, TS])
        cs_den = sb("cs_den", [P, TS])
        cs_inv = sb("cs_inv", [P, TS])
        rs_is0 = sb("rs_is0", [P, T])
        c1_raw = sb("c1_raw", [P, T])
        c1_safe = sb("c1_safe", [P, T])
        c1_ok = sb("c1_ok", [P, T])
        c1 = sb("c1", [P, T])
        stats = sb("stats", [P, 2, GT, 6])
        meanvar = sb("meanvar", [P, 2, GT, 2])
        var_eps = sb("var_eps", [P, 2, GT])
        rstd = sb("rstd", [P, 2, GT])
        minus_half = sb("minus_half", [P, GT])

        psP = ctx.enter_context(nc.psum_tensor("psP", [P, 2, BANK], F32))
        psT = ctx.enter_context(nc.psum_tensor("psT", [P, 2, BANK], F32))
        psQ = ctx.enter_context(nc.psum_tensor("psQ", [P, 2, BANK], F32))
        psE = ctx.enter_context(nc.psum_tensor("psE", [P, 2, BANK], F32))

        raw_in = [sem(f"raw_in{s}") for s in range(NRAW)]
        keep_in = sem("keep_in")
        x_loaded = [sem(f"x_loaded{q}") for q in range(SL)]
        w_in_sem = sem("weights_loaded")
        ident_ok = sem("ident_ok")
        ident_zero = sem("ident_zero")
        nat_hi = sem("nat_hi")
        nat_lo = sem("nat_lo")
        nat_used = sem("nat_used")
        t_done = sem("t_done")
        t_out = sem("t_out")
        t_hi = sem("t_hi")
        t_hi_act = sem("t_hi_act")
        t_lo = sem("t_lo")
        t_used = sem("t_used")
        stored = [sem(f"stored{h}") for h in range(2)]
        acc_zero = sem("acc_zero")
        q_added = sem("q_added")
        hj_ok = sem("hj_ok")
        cs_sum = sem("cs_sum")
        rs_sum = sem("rs_sum")
        cs_step = sem("cs_step")
        cs_den_ok = sem("cs_den_ok")
        cs_inv_ok = sem("cs_inv_ok")
        rs_step = sem("rs_step")
        rs_den_ok = sem("rs_den_ok")
        rs_inv_ok = sem("rs_inv_ok")
        c1_step = sem("c1_step")
        a_hi = sem("a_hi")
        a_lo = sem("a_lo")
        a_used = sem("a_used")
        p_half = sem("p_half")
        p_out = sem("p_out")
        e_done = sem("e_done")
        e_used = sem("e_used")
        ln_stats = sem("ln_stats")
        ln_mv = sem("ln_mv")
        ln_eps = sem("ln_eps")
        ln_rstd = sem("ln_rstd")
        half_ok = sem("half_ok")
        hn_ok = sem("hn_ok")
        pool_late = sem("pool_late")
        hs_hi = sem("hs_hi")
        hs_lo = sem("hs_lo")
        ht_done = sem("ht_done")
        ht_out = sem("ht_out")
        g_done = sem("g_done")
        g_used = sem("g_used")
        part_out = sem("part_out")
        y_ok = sem("y_ok")
        o_ok = sem("o_ok")
        o_out = sem("o_out")

        def f32(ap):
            return ap.bitcast(F32)

        def cols(t, first, n):
            return t[:, bass.ds(first, n)]

        def base(p):
            return T * SL * (p - 1)

        RAW_PASS0 = [16 * SL * SUP // 2 if s < RING0 else 0 for s in range(NRAW)]
        RAW_CHUNK = PAIRS // NRAW * 16

        def slot(m):
            return (m + RING0) % NRAW

        def raw_count(kk):
            return RAW_PASS0[slot(kk)] + (kk // NRAW + 1) * 16

        def raw_visit(m):
            return SL * RAW_CHUNK + raw_count(m)

        def tile1(oc, k):
            if k < KEEP:
                return keep[:, k, bass.ds(oc * WIDE, WIDE)]
            return raw[:, slot((k - KEEP) // 2), k % 2, :]

        def tile2(n):
            return raw[:, slot(n // 2), n % 2, :]

        def nat_tile(r, first=0, n=WIDE):
            return raw[:, (r // 2) % RING0, r % 2, first:first + n]

        def nat_landed(J, r):
            return raw_in[(r // 2) % RING0], (J * SUP // 2 if isinstance(J, int) else J * (SUP // 2)) * 16 + (r // 8 + 1) * 16

        def t_dst(q):
            return stage[:, q % 4, :, :]

        def hn_view(g):
            return acc[:, g * BANK:(g + 1) * BANK]

        def hi_on_act(q, last):
            return q % 4 != 0 if last else q % 2 == 1

        ACT_HI = SLOTS // 2
        LN0, LN1, LN2, LN3 = 0, NG, 2 * NG, 3 * NG
        E0 = 2 * SL + NG

        VISITS = [
            (2, 0, (0, 1, 2, 3), ()), (2, 1, (1, 2, 3, 0), (0,)),
            (2, 2, (2, 3, 0, 1), (0, 1)), (2, 3, (3, 0, 1, 2), (0, 1, 2)),
            (3, 2, (2, 3), ()), (3, 3, (3,), ()), (3, 1, (1, 2, 3), (2, 3)), (3, 0, (0, 2, 3, 1), (1, 2, 3)),
            (4, 3, (3, 2, 1, 0), ()), (4, 2, (3, 2, 1, 0), ()), (4, 1, (1, 0), ()), (4, 0, (0,), ())]
        TILES = [(v, J * TS + j) for v, visit in enumerate(VISITS) for J in visit[2] for j in range(TS)]
        END = [sum(TS * len(visit[2]) for visit in VISITS[:v + 1]) for v in range(len(VISITS))]
        LAST2 = 3
        HOP2 = 8
        TAIL = 19
        BOTH = [v for v, visit in enumerate(VISITS) if visit[3]]
        PARTS = [v for v, (p, c, Js, both) in enumerate(VISITS) if len(Js) < SL]
        NEVER = (-1000, -1000)
        STEPS2 = dict(copy=(1, 1), rows=(4, 5), add=(6, 7), stats=(8, 9), aggregate=(10, 11), 
                      split=(17, 19), silu=NEVER, out=NEVER, store=NEVER)
        STEPS3 = dict(copy=(1, 1), rows=(4, 5), add=(6, 7), stats=NEVER, aggregate=NEVER, 
                      split=(12, 14), silu=(8, 10), out=(12, 14), store=(16, 18))
        SOONER = dict(STEPS2, copy=(1, 1), rows=(1, 2), add=(3, 4), stats=(4, 5), aggregate=(5, 6),
                      split=(8, 9))

        def due(n, step, i):
            for v in range(len(VISITS)):
                steps = STEPS2 if v < LAST2 else SOONER if v == LAST2 else STEPS3
                if n == END[v] + steps[step][i]:
                    return v
            return None

        def split_count(p, k):
            if p == 2:
                return NG * 2 + k // GT + 1
            made = [c for q, c, Js, both in VISITS if q == p - 1].index(k // TS)
            return NG * p + 2 * made + k % TS // GT + 1

        def chunks_done(v):
            return 2 * SL + v + 1

        def e_index(v, i):
            return E0 + 2 * (SL + v) + i

        def y_view(i):
            return stage[:, 2 + i, 0, :]

        def z_view(i):
            return stage[:, i, 1, :]

        def norm_view(i):
            return stage[:, i, 0, :]

        block = ctx.enter_context(nc.Block())

        @block.sync
        def _(sp):
            def load_super(J, I, guard):
                for half in range(2):
                    s = (2 * I + half) % RING0
                    if guard and half == 0:
                        sp.wait_ge(nat_used, J * SLOTS + I * 4 - 4)
                    sp.dma_start(raw[:, s, :, :],
                                 adj_t[:, 4 * I + 2 * half:4 * I + 2 * half + 2, bass.ds(J * WIDE, WIDE)]
                                 ).then_inc(raw_in[s], 16)

            def store_half(J, I, h):
                sp.wait_ge(t_out, (J * SLOTS + 4 * I + 2 * h + 2) * 2)
                src = stage[:, 2 * h:2 * h + 2, :, :].rearrange("p u b c -> p (u b) c")
                sp.dma_start(adjT_v[:, I // 2, bass.ds(J * TS + 4 * h, 4), (I % 2) * BANK:(I % 2 + 1) * BANK],
                             src).then_inc(stored[h], 16)

            def load_pair(oc, kk):
                sp.dma_start(raw[:, slot(kk), :, :], adj_t[:, KEEP + 2 * kk:KEEP + 2 * kk + 2, bass.ds(oc * WIDE, WIDE)]
                             ).then_inc(raw_in[slot(kk)], 16)

            def slab(J, first=False, last=False):
                for I in range(SUP):
                    if I + 1 < SUP:
                        load_super(J, I + 1, guard=not (first and I == 0))
                    elif not last:
                        load_super(J + 1, 0, guard=True)
                    if last and 1 <= I <= SL:
                        sp.dma_start(keep[:, :, (I - 1) * WIDE:I * WIDE],
                                     adj_t[:, 0:KEEP, (I - 1) * WIDE:I * WIDE]).then_inc(keep_in, 16)
                    if last and I == SUP - 2:
                        load_pair(0, 0)
                    if last and I == SUP - 1:
                        sp.wait_ge(nat_used, SL * SLOTS - 4)
                        load_pair(0, 1)
                        load_pair(0, 2)
                    store_half(J, I, 0)
                    store_half(J, I, 1)

            sp.dma_start(x[:, 0:BANK].rearrange("p (t d) -> p t d", d=P), x_t[:, 0:GT, :]).then_inc(x_loaded[0], 16)
            sp.dma_start(x[:, BANK:WIDE].rearrange("p (t d) -> p t d", d=P), x_t[:, GT:TS, :]).then_inc(x_loaded[1], 16)
            load_super(0, 0, guard=False)
            sp.dma_start(x[:, WIDE:2 * WIDE].rearrange("p (t d) -> p t d", d=P), x_t[:, TS:2 * TS, :]).then_inc(x_loaded[2], 16)
            sp.dma_start(x[:, 2 * WIDE:].rearrange("p (t d) -> p t d", d=P), x_t[:, 2 * TS:, :]).then_inc(x_loaded[3], 16)
            for w, src in ((wi, w_in), (wo, w_out), (w2a, w_l2[0:P, :]), (w2b, w_l2[P:2 * P, :]), (w3, w_l3)):
                sp.dma_start(w[:, :], src).then_inc(w_in_sem, 16)
            sp.dma_start(b3[:, :], b_l3.partition_broadcast(P)).then_inc(w_in_sem, 16)
            slab(0, first=True)
            with sp.Fori(1, SL - 1) as J:
                slab(J)
            slab(SL - 1, last=True)

            def load_chunk(oc, lead):
                for kk in range(PAIRS):
                    if lead and kk < 3:
                        continue
                    if lead and kk < NRAW:
                        if kk == 3:
                            sp.wait_ge(nat_used, SL * SLOTS)
                    elif kk >= NRAW:
                        sp.wait_ge(a_lo, oc * T + KEEP + 2 * (kk - NRAW) + 2)
                    else:
                        sp.wait_ge(a_lo, oc * T - T + KEEP + 2 * (kk + PAIRS - NRAW) + 2)
                    load_pair(oc, kk)

            load_chunk(0, True)
            with sp.Fori(1, SL) as oc:
                load_chunk(oc, False)

            for h in range(2):
                sp.wait_ge(stored[h], 16 * SL * SUP)
            for m in range(len(TILES) // 2):
                if m >= NRAW:
                    sp.wait_ge(a_lo, base(2) + 2 * (m - NRAW) + 2)
                else:
                    sp.wait_ge(a_lo, base(2) - T + KEEP + 2 * (m + PAIRS - NRAW) + 2)
                v, k = TILES[2 * m]
                sp.dma_start(raw[:, slot(m), :, :], adjT_v[:, VISITS[v][1], k:k + 2, :]).then_inc(raw_in[slot(m)], 16)

        @block.gpsimd
        def _(pool):
            pool.memset(ident[:, :], 0.0).then_inc(ident_zero, 1)
            pool.wait_ge(ident_zero, 1)
            pool.affine_select(out=ident[:, :], in_=ident[:, :], compare_op=ALU.not_equal, fill=1.0,
                               base=0, pattern=[[-1, P]], channel_multiplier=1).then_inc(ident_ok, 1)

            pool.memset(minus_half[:, :], -0.5).then_inc(half_ok, 1)
            pool.wait_ge(half_ok, 1)

            def norm_factors(i, index):
                pool.wait_ge(ln_mv, index + 1)
                pool.tensor_scalar(var_eps[:, i, :], meanvar[:, i, :, 1], EPS, None, op0=ALU.add).then_inc(ln_eps, 1)
                pool.wait_ge(ln_eps, index + 1)
                pool.tensor_tensor(rstd[:, i, :], var_eps[:, i, :], minus_half[:, :], ALU.pow).then_inc(ln_rstd, 1)

            def normalise(i, index, first_col, dst, first_dst):
                norm_factors(i, index)
                pool.wait_ge(ln_rstd, index + 1)
                for t in range(GT):
                    ins = pool.tensor_scalar(dst[:, first_dst + t * P:first_dst + (t + 1) * P],
                                             x[:, first_col + t * P:first_col + (t + 1) * P],
                                             meanvar[:, i, t, 0:1], rstd[:, i, t:t + 1],
                                             op0=ALU.subtract, op1=ALU.mult)
                ins.then_inc(hn_ok, 1)

            def slab(J):
                pool.wait_ge(cs_sum, J + 1)
                pool.tensor_scalar(cs_pos[:, :], cols(cs, J * TS, TS), 0.0, None, op0=ALU.max).then_inc(cs_step, 1)
                pool.tensor_scalar(cs_is0[:, :], cols(cs, J * TS, TS), 0.0, None, op0=ALU.is_le).then_inc(cs_step, 1)
                pool.wait_ge(cs_step, 2 * (J + 1))
                if J > 0:
                    pool.wait_ge(cs_inv_ok, J)
                pool.tensor_tensor(cs_den[:, :], cs_pos[:, :], cs_is0[:, :], ALU.add).then_inc(cs_den_ok, 1)

            for g in range(NG):
                norm_factors(g % 2, LN0 + g)
            slab(0)
            for J in range(1, SL - 1):
                slab(J)
            for I in range(SUP):
                if I >= 2:
                    G = I - 2
                    normalise(G % 2, LN1 + G, G * BANK, acc, G * BANK)
                r = slice(GT * I, GT * I + GT)
                pool.wait_ge(rs_sum, I + 1)
                pool.tensor_scalar(rs_pos[:, r], rs[:, r], 0.0, None, op0=ALU.max).then_inc(rs_step, 1)
                pool.tensor_scalar(rs_is0[:, r], rs[:, r], 0.0, None, op0=ALU.is_le).then_inc(rs_step, 1)
                pool.wait_ge(rs_step, 2 * I + 2)
                pool.tensor_tensor(rs_den[:, r], rs_pos[:, r], rs_is0[:, r], ALU.add).then_inc(rs_den_ok, 1)
            slab(SL - 1)
            for G in range(NG - 2, NG):
                norm_factors(G % 2, LN1 + G)
            pool.wait_ge(c1_step, 3)
            pool.tensor_tensor(c1[:, :], c1_safe[:, :], c1_ok[:, :], ALU.mult).then_inc(pool_late, 1)

            def keep_normed(c):
                for i in range(2):
                    n = 2 * (c - 1) + i
                    pool.wait_ge(hn_ok, LN2 + n + 1)
                    pool.tensor_copy(cols(acc, n * BANK, BANK), pt[:, i * BANK:(i + 1) * BANK]).then_inc(pool_late, 1)

            for c in range(SL):
                for i in range(2):
                    if c < SL - 1:
                        normalise(i, LN2 + 2 * c + i, c * WIDE + i * BANK, pt, i * BANK)
                    else:
                        norm_factors(i, LN2 + 2 * c + i)
                keep_normed(c + 1)
            stage_cols = stage[:, :, :, :].rearrange("p u b c -> p (u b c)")
            for v in range(LAST2 + 1):
                for i in range(2):
                    if v < LAST2:
                        normalise(i, LN3 + 2 * v + i, VISITS[v][1] * WIDE + i * BANK, stage_cols, 2 * i * BANK)
                    else:
                        norm_factors(i, LN3 + 2 * v + i)

        @block.scalar
        def _(act):
            def split_h(g, src, index, func):
                if index >= LN2:
                    act.wait_ge(pool_late, 1 + g + 1)
                else:
                    act.wait_ge(hn_ok, index + 1)
                act.activation(h_hi[:, g * BANK:(g + 1) * BANK], src, func).then_inc(hs_hi, 1)

            def split_group(p, g):
                split_h(g, hn_view(g), NG * p + g, ACT.Relu)

            def natural_hi(J, q, first):
                g = J * SLOTS + q
                if q % 2 == 0:
                    act.wait_ge(*nat_landed(J, q))
                if not (first and q < 2):
                    act.wait_ge(nat_used, g - 1)
                act.activation(hi[:, q % 2, :], nat_tile(q), ACT.Copy,
                               accum_out=rs_part[:, bass.ds(J, 1), q:q + 1].rearrange("p a b -> p (a b)")).then_inc(nat_hi, 1)

            def slab(J, first=False, last=False):
                natural_hi(J, 0, first)
                if not first:
                    for b in range(2):
                        if b == 0:
                            act.wait_ge(p_half, J)
                        else:
                            act.wait_ge(nat_used, J * SLOTS)
                        act.activation(pt[:, b * BANK:(b + 1) * BANK], psP[:, b, :], ACT.Copy).then_inc(p_out, 1)
                    act.wait_ge(cs_sum, J)
                for q in range(SLOTS):
                    g = J * SLOTS + q
                    u = q % 4
                    if q + 1 < SLOTS:
                        natural_hi(J, q + 1, first)
                    if not (first and q < 4):
                        act.wait_ge(stored[u // 2], 16 * (J * SUP + q // 4))
                        act.wait_ge(t_lo, g - 3)
                    for b in range(2):
                        act.wait_ge(t_done, 2 * g + b + 1)
                        act.activation(t_dst(q)[:, b, :], psT[:, b, :], ACT.Copy,
                                       accum_out=cs_part[:, 2 * u + b, q // 4:q // 4 + 1]).then_inc(t_out, 1)
                    if hi_on_act(q, last):
                        act.wait_ge(t_out, 2 * g + 2)
                        if not (first and q < 2):
                            act.wait_ge(t_used, g - 1)
                        act.activation(hi[:, 2 + q % 2, :].rearrange("p (b c) -> p b c", b=2), t_dst(q),
                                       ACT.Copy).then_inc(t_hi_act, 1)
                    if last and u == 1 and q // 4 >= 3:
                        split_group(1, q // 4 - 3)
                    if first and q % 4 == 1 and 1 <= q // 4 <= NG - 2:
                        n = q // 4 + 1
                        split_h(n, pt[:, n % 2 * BANK:(n % 2 + 1) * BANK], LN0 + n, ACT.Relu)

            for g in range(2):
                split_h(g, pt[:, g * BANK:(g + 1) * BANK], LN0 + g, ACT.Relu)
            slab(0, first=True)
            with act.Fori(1, SL - 1) as J:
                slab(J)
            slab(SL - 1, last=True)

            def copy_product(count, ready):
                for b in range(2):
                    if b == 0:
                        act.wait_ge(p_half, count)
                    else:
                        act.wait_ge(*ready)
                    act.activation(pt[:, b * BANK:(b + 1) * BANK], psP[:, b, :], ACT.Copy).then_inc(p_out, 1)

            def lead_splits(p, k):
                if p == 1 and k == 2:
                    split_group(p, NG - 3)
                if k in (18, 21):
                    split_group(p, NG - 2 + (k == 21))

            def transposed_norms(c, k):
                for i in range(2):
                    if k == 18 + 2 * i:
                        act.wait_ge(ht_done, 2 * (c - 1) + i + 1)
                        act.activation(norm_view(i), psT[:, i, :], ACT.Relu).then_inc(ht_out, 1)

            def chunk(oc, lead=False, last=False):
                for k in range(T):
                    n = oc * T + k
                    if k % 2 == 0 and k >= KEEP:
                        kk = (k - KEEP) // 2
                        act.wait_ge(raw_in[slot(kk)], oc * RAW_CHUNK + raw_count(kk))
                    if lead and k == 0:
                        act.wait_ge(keep_in, 16 * SL)
                    if lead and k < 4:
                        if k == 0:
                            act.wait_ge(nat_used, SL * SLOTS)
                        if k == 2:
                            act.wait_ge(t_used, SL * SLOTS)
                    else:
                        act.wait_ge(a_used, n - 3)
                    act.activation(hi[:, k % 4, :], tile1(oc, k), ACT.Copy).then_inc(a_hi, 1)
                    if k == 1:
                        if lead:
                            copy_product(SL, (nat_used, SL * SLOTS))
                        else:
                            act.wait_ge(pool_late, 2 * oc - 1)
                            copy_product(SL + oc, (a_used, oc * T))
                    if lead:
                        lead_splits(1, k)
                    else:
                        transposed_norms(oc, k)
                    if last and k % GT == 0 and 2 <= k // GT < NG:
                        split_group(2, k // GT - 2)
                if lead:
                    for h in range(2):
                        act.wait_ge(stored[h], 16 * SL * SUP)

            chunk(0, lead=True)
            with act.Fori(1, SL - 1) as oc:
                chunk(oc)
            chunk(SL - 1, last=True)

            for n in range(len(TILES) + TAIL):
                if n < len(TILES):
                    if n % 2 == 0:
                        act.wait_ge(raw_in[slot(n // 2)], raw_visit(n // 2))
                    act.wait_ge(a_used, base(2) + n - 3)
                    act.activation(hi[:, n % 4, :], tile2(n), ACT.Copy).then_inc(a_hi, 1)
                if n < T:
                    if n == 1:
                        act.wait_ge(pool_late, 2 * SL - 1)
                        copy_product(2 * SL, (a_used, base(2)))
                    lead_splits(2, n)
                    transposed_norms(SL, n)
                v = due(n, "copy", 0)
                if v is not None:
                    if v not in PARTS:
                        copy_product(chunks_done(v), (a_used, base(2) + END[v]))
                    if v in BOTH:
                        c = VISITS[v][1]
                        if v in PARTS:
                            act.wait_ge(p_out, 2 * chunks_done(v))
                        if v == BOTH[0]:
                            act.wait_ge(hs_lo, 3 * NG)
                        act.wait_ge(a_used, base(2) + END[v])
                        for b in range(2):
                            act.activation(acc[:, c * WIDE + b * BANK:c * WIDE + (b + 1) * BANK], psQ[:, b, :],
                                           ACT.Copy).then_inc(part_out, 1)
                for i in range(2):
                    v = due(n, "silu", i)
                    if v is not None:
                        act.wait_ge(e_used, e_index(v, i) + 1)
                        act.activation(y_view(i), z_view(i), ACT.Silu).then_inc(y_ok, 1)
                    v = due(n, "split", i)
                    if v is not None and v < HOP2:
                        g = 2 * VISITS[v][1] + i
                        gs = slice(g * BANK, (g + 1) * BANK)
                        if v <= LAST2:
                            act.wait_ge(hn_ok, LN3 + 2 * v + i + 1)
                            act.activation(g_hi[:, gs], norm_view(i), ACT.Relu).then_inc(hs_hi, 1)
                        else:
                            act.wait_ge(y_ok, 2 * (v - LAST2 - 1) + i + 1)
                            act.activation(h_hi[:, gs], y_view(i), ACT.Copy).then_inc(hs_hi, 1)
                    v = due(n, "store", i)
                    if v is not None and v >= HOP2:
                        g = 2 * VISITS[v][1] + i
                        act.wait_ge(o_ok, 2 * (v - HOP2) + i + 1)
                        act.dma_start(out_t[:, g * GT:(g + 1) * GT, :],
                                      x[:, g * BANK:(g + 1) * BANK].rearrange("p (t d) -> p t d", d=P)).then_inc(o_out, 16)
            act.wait_ge(o_out, 16 * NG)

        @block.vector
        def _(dve):
            def ln_a(i, rows):
                for t in range(GT):
                    ins = dve.bn_stats(stats[:, i, t, :], rows(t))
                ins.then_inc(ln_stats, 1)

            def ln_b(i):
                for t in range(GT):
                    ins = dve.bn_aggr(meanvar[:, i, t, :], stats[:, i, t, :])
                ins.then_inc(ln_mv, 1)

            def ln_d(i, index, rows, dst):
                dve.wait_ge(ln_rstd, index + 1)
                for t in range(GT):
                    ins = dve.tensor_scalar(dst(t), rows(t), meanvar[:, i, t, 0:1], rstd[:, i, t:t + 1],
                                            op0=ALU.subtract, op1=ALU.mult)
                ins.then_inc(hn_ok, 1)

            def split_h(g, src, index, relu):
                dve.wait_ge(hs_hi, index + 1)
                gs = slice(g * BANK, (g + 1) * BANK)
                if relu:
                    dve.scalar_tensor_tensor(h_lo[:, gs], src, 0.0, f32(h_hi[:, gs]), op0=ALU.max, op1=ALU.subtract).then_inc(hs_lo, 1)
                else:
                    dve.tensor_tensor(h_lo[:, gs], src, f32(h_hi[:, gs]), ALU.subtract).then_inc(hs_lo, 1)

            def split_group(p, g):
                split_h(g, hn_view(g), NG * p + g, True)

            def x_rows(first_col):
                return lambda t: cols(x, first_col + t * P, P) if not isinstance(first_col, int) \
                    else x[:, first_col + t * P:first_col + (t + 1) * P]

            def scaled_add(e, bank, first_col, inv):
                dve.wait_ge(e_done, e + 1)
                xr = x_rows(first_col)
                for t in range(GT):
                    ins = dve.scalar_tensor_tensor(xr(t), psE[:, bank, t * P:(t + 1) * P], inv(t), xr(t),
                                                   op0=ALU.mult, op1=ALU.add)
                ins.then_inc(e_used, 1)

            def first_rows(g):
                return x_rows(g * BANK)

            def first_hn(g):
                return lambda t: pt[:, (g % 2) * BANK + t * P:(g % 2) * BANK + (t + 1) * P]

            def first_step(g, step):
                i = g % 2
                if step == 0:
                    dve.wait_ge(x_loaded[min(g, 2) if g < 4 else 3], 16)
                    ln_a(i, first_rows(g))
                if step == 1:
                    dve.wait_ge(ln_stats, g + 1)
                    ln_b(i)
                if step == 3:
                    if g >= 2:
                        dve.wait_ge(hs_lo, g - 1)
                    ln_d(i, g, first_rows(g), first_hn(g))

            def natural_lo(J, q):
                g = J * SLOTS + q
                dve.wait_ge(nat_hi, g + 1)
                dve.tensor_tensor(lo[:, q % 2, :], nat_tile(q), f32(hi[:, q % 2, :]), ALU.subtract).then_inc(nat_lo, 1)

            def add_q(J, I, first):
                dve.wait_ge(t_used, J * SLOTS + 4 * I + 4)
                a = acc[:, I * BANK:(I + 1) * BANK]
                if first and I < SUP - 1:
                    dve.tensor_copy(a, psQ[:, I % 2, :]).then_inc(q_added, 1)
                else:
                    if I == SUP - 1:
                        dve.wait_ge(acc_zero, 1)
                    dve.wait_ge(q_added, J * SUP + I + 1 - SUP if I < SUP - 1 else J * SUP + I)
                    dve.tensor_tensor(a, psQ[:, I % 2, :], a, ALU.add).then_inc(q_added, 1)

            def slab(J, first=False, last=False):
                if not first and not last:
                    dve.wait_ge(t_used, J * SLOTS)
                    dve.tensor_copy(hj_hi[:, :], f32(cols(h_hi, J * WIDE, WIDE)))
                    dve.tensor_copy(hj_lo[:, :], f32(cols(h_lo, J * WIDE, WIDE))).then_inc(hj_ok, 1)
                natural_lo(J, 0)
                for q in range(SLOTS):
                    g = J * SLOTS + q
                    I, u = q // 4, q % 4
                    ring_t = 2 + q % 2
                    if q + 1 < SLOTS:
                        natural_lo(J, q + 1)
                    by_act = hi_on_act(q, last)
                    if not by_act:
                        dve.wait_ge(t_out, 2 * g + 2)
                        if not (first and q < 2):
                            dve.wait_ge(t_used, g - 1)
                    hi_t = hi[:, ring_t, :].rearrange("p (b c) -> p b c", b=2)
                    lo_t = lo[:, ring_t, :].rearrange("p (b c) -> p b c", b=2)
                    if not by_act:
                        dve.tensor_copy(hi_t, t_dst(q)).then_inc(t_hi, 1)
                    if u == 2 and I >= 1:
                        add_q(J, I - 1, first)
                    if first and I + 2 < NG:
                        first_step(I + 2, u)
                    if first and u == 2 and 1 <= I <= NG - 2:
                        n = I + 1
                        split_h(n, pt[:, n % 2 * BANK:(n % 2 + 1) * BANK], LN0 + n, True)
                    if not first:
                        if q == 1:
                            add_q(J - 1, SUP - 1, False)
                            dve.wait_ge(cs_den_ok, J)
                            dve.reciprocal(cs_inv[:, :], cs_den[:, :]).then_inc(cs_inv_ok, 1)
                        if q in (4, 5):
                            i = q - 4
                            if i == 0:
                                dve.wait_ge(cs_inv_ok, J)
                            scaled_add(2 * (J - 1) + i, i, J * WIDE - WIDE + i * BANK,
                                       lambda t, i=i: cs_inv[:, i * GT + t:i * GT + t + 1])
                    n_act = J * ACT_HI + sum(hi_on_act(r, last) for r in range(q + 1))
                    n_dve = J * (SLOTS - ACT_HI) + sum(not hi_on_act(r, last) for r in range(q + 1))
                    if by_act:
                        dve.wait_ge(t_hi_act, n_act)
                    else:
                        dve.wait_ge(t_hi, n_dve)
                    dve.tensor_tensor(lo_t, t_dst(q), f32(hi_t), ALU.subtract).then_inc(t_lo, 1)
                    if last and u == 1 and I >= 3:
                        split_group(1, I - 3)
                    if last:
                        if u == 0 and I >= 2:
                            row_update(I - 2)
                        if u >= 1 and I >= 2:
                            ln_group(I - 2, u - 1)
                        if u == 2 and I >= 1:
                            row_factors(I - 1)
                        if u == 3:
                            dve.wait_ge(nat_hi, J * SLOTS + q + 1)
                            part = rs_part[:, :, GT * I:GT * I + GT].rearrange("p s t -> p t s")
                            dve.reduce_sum(rs[:, GT * I:GT * I + GT], part, axis=AX.X).then_inc(rs_sum, 1)
                dve.wait_ge(t_out, J * SLOTS * 2 + SLOTS * 2)
                dve.reduce_sum(cols(cs, J * TS, TS), cs_part[:, :, :], axis=AX.X).then_inc(cs_sum, 1)

            def row_factors(G):
                dve.wait_ge(rs_den_ok, G + 1)
                r = slice(G * GT, (G + 1) * GT)
                dve.reciprocal(rs_inv[:, r], rs_den[:, r]).then_inc(rs_inv_ok, 1)

            def row_update(G):
                dve.wait_ge(rs_inv_ok, G + 1)
                scaled_add(2 * (SL - 1) + G, G % 2, G * BANK,
                           lambda t: rs_inv[:, G * GT + t:G * GT + t + 1])

            def ln_group(G, step):
                if step == 0:
                    dve.wait_ge(e_used, 2 * (SL - 1) + G + 1)
                    ln_a(G % 2, x_rows(G * BANK))
                if step == 1:
                    dve.wait_ge(ln_stats, LN1 + G + 1)
                    dve.wait_ge(hn_ok, LN1 + G - 1)
                    ln_b(G % 2)

            dve.memset(acc[:, N - BANK:], 0.0).then_inc(acc_zero, 1)
            for g in range(2):
                for step in range(4):
                    first_step(g, step)
                split_h(g, pt[:, g * BANK:(g + 1) * BANK], LN0 + g, True)
            slab(0, first=True)
            with dve.Fori(1, SL - 1) as J:
                slab(J)
            slab(SL - 1, last=True)

            def last_of_pass0(k):
                if k == 0:
                    add_q(SL - 1, SUP - 1, False)
                    row_factors(NG - 1)
                if k == 4:
                    dve.wait_ge(cs_den_ok, SL)
                    dve.reciprocal(cs_inv[:, :], cs_den[:, :]).then_inc(cs_inv_ok, 1)
                    dve.wait_ge(cs_sum, SL)
                    dve.reciprocal(c1_raw[:, :], cs[:, :]).then_inc(c1_step, 1)
                if k == 10:
                    dve.wait_ge(c1_step, 1)
                    dve.tensor_scalar(c1_safe[:, :], c1_raw[:, :], FLT_MAX, -FLT_MAX, op0=ALU.min, op1=ALU.max).then_inc(c1_step, 1)
                if k == 11:
                    dve.wait_ge(c1_step, 2)
                    dve.tensor_tensor(c1_ok[:, :], c1_safe[:, :], c1_raw[:, :], ALU.is_equal).then_inc(c1_step, 1)
                if k == 5:
                    row_update(NG - 2)
                    row_update(NG - 1)
                if k == 6:
                    dve.wait_ge(cs_inv_ok, SL)
                    dve.wait_ge(e_used, 2 * (SL - 1) + NG)
                for i in range(2):
                    col = N - WIDE + i * BANK
                    if k == 6 + i:
                        scaled_add(2 * SL + NG - 2 + i, i, col, lambda t: cs_inv[:, i * GT + t:i * GT + t + 1])
                    if k == 8 + i:
                        ln_a(i, x_rows(col))
                    if k == 10 + i:
                        ln_b(i)
                    if k == 13 + i:
                        ln_d(i, LN1 + NG - 2 + i, x_rows(col), lambda t: acc[:, col + t * P:col + (t + 1) * P])

            def last_chunk(c, k):
                for i in range(2):
                    col = (c - 1) * WIDE + i * BANK
                    if k == 6 + i:
                        if i == 0:
                            dve.wait_ge(pool_late, 1)
                        scaled_add(E0 + 2 * (c - 1) + i, i, col, lambda t: cols(c1, (c - 1) * TS + i * GT + t, 1))
                    if k == 8 + i:
                        ln_a(i, x_rows(col))
                    if k == 10 + i:
                        ln_b(i)
                    if k == 22 + 2 * i:
                        dve.wait_ge(g_done, 2 * (c - 1) + i + 1)
                        dve.tensor_tensor(cols(x, col, BANK), psQ[:, i, :], cols(x, col, BANK), ALU.add).then_inc(g_used, 1)

            def norm_waits(e, ln, k):
                for i in range(2):
                    if k == 8 + i:
                        dve.wait_ge(e_used, e + i + 1)
                    if k == 10 + i:
                        dve.wait_ge(ln_stats, ln + i + 1)

            def lead_splits(p, k):
                if p == 1 and k == 2:
                    split_group(p, NG - 3)
                if k in (18, 21):
                    split_group(p, NG - 2 + (k == 21))

            def chunk(oc, lead=False, last=False):
                for k in range(T):
                    if lead:
                        norm_waits(2 * SL + NG - 2, LN1 + NG - 2, k)
                    else:
                        norm_waits(E0 + 2 * (oc - 1), LN2 + 2 * (oc - 1), k)
                    dve.wait_ge(a_hi, oc * T + k + 1)
                    dve.tensor_tensor(lo[:, k % 4, :], tile1(oc, k), f32(hi[:, k % 4, :]),
                                      ALU.subtract).then_inc(a_lo, 1)
                    if lead:
                        lead_splits(1, k)
                        last_of_pass0(k)
                    else:
                        last_chunk(oc, k)
                    if last and k % GT == 0 and 2 <= k // GT < NG:
                        split_group(2, k // GT - 2)

            chunk(0, lead=True)
            with dve.Fori(1, SL - 1) as oc:
                chunk(oc)
            chunk(SL - 1, last=True)

            for n in range(len(TILES) + TAIL):
                if n < T:
                    norm_waits(E0 + 2 * (SL - 1), LN2 + 2 * (SL - 1), n)
                for i in range(2):
                    v = due(n, "stats", i)
                    if v is not None:
                        dve.wait_ge(e_used, e_index(v, i) + 1)
                    v = due(n, "aggregate", i)
                    if v is not None:
                        dve.wait_ge(ln_stats, LN3 + 2 * v + i + 1)
                if n < len(TILES):
                    dve.wait_ge(a_hi, base(2) + n + 1)
                    dve.tensor_tensor(lo[:, n % 4, :], tile2(n), f32(hi[:, n % 4, :]),
                                      ALU.subtract).then_inc(a_lo, 1)
                if n < T:
                    lead_splits(2, n)
                    last_chunk(SL, n)
                    for i in range(2):
                        if n == 13 + i:
                            ln_d(i, LN2 + 2 * (SL - 1) + i, x_rows(N - WIDE + i * BANK),
                                 lambda t: pt[:, i * BANK + t * P:i * BANK + (t + 1) * P])
                v = due(n, "copy", 0)
                if v is not None and v in PARTS:
                    c = VISITS[v][1]
                    dve.wait_ge(part_out, 2 * (BOTH.index(max(w for w in BOTH if VISITS[w][1] == c and w < v)) + 1))
                    for b in range(2):
                        if b == 0:
                            dve.wait_ge(p_half, chunks_done(v))
                        else:
                            dve.wait_ge(a_used, base(2) + END[v])
                        bs = slice(b * BANK, (b + 1) * BANK)
                        dve.tensor_tensor(pt[:, bs], psP[:, b, :], acc[:, c * WIDE + b * BANK:c * WIDE + (b + 1) * BANK],
                                          ALU.add).then_inc(p_out, 1)
                for i in range(2):
                    v = due(n, "add", i)
                    if v is not None:
                        col = VISITS[v][1] * WIDE + i * BANK
                        dve.wait_ge(e_done, e_index(v, i) + 1)
                        if v <= LAST2:
                            dve.wait_ge(g_used, 2 * SL)
                            dve.tensor_tensor(x[:, col:col + BANK], psE[:, i, :], x[:, col:col + BANK], ALU.add).then_inc(e_used, 1)
                        else:
                            z = z_view(i).rearrange("p (t d) -> p t d", d=P)
                            row = psE[:, i, :].rearrange("p (t d) -> p t d", d=P)
                            dve.tensor_tensor(z, row, b3[:, :].unsqueeze(1).broadcast_to([P, GT, P]), ALU.add).then_inc(e_used, 1)
                    v = due(n, "stats", i)
                    if v is not None:
                        ln_a(i, x_rows(VISITS[v][1] * WIDE + i * BANK))
                    v = due(n, "aggregate", i)
                    if v is not None:
                        ln_b(i)
                    if n == END[LAST2] + 7 + i:
                        ln_d(i, LN3 + 2 * LAST2 + i, x_rows(VISITS[LAST2][1] * WIDE + i * BANK),
                             lambda t: stage[:, i, 0, t * P:(t + 1) * P])
                    v = due(n, "split", i)
                    if v is not None and v < HOP2:
                        dve.wait_ge(hs_hi, 3 * NG + 2 * v + i + 1)
                        g = 2 * VISITS[v][1] + i
                        gs = slice(g * BANK, (g + 1) * BANK)
                        if v <= LAST2:
                            dve.scalar_tensor_tensor(g_lo[:, gs], norm_view(i), 0.0, f32(g_hi[:, gs]), op0=ALU.max,
                                                     op1=ALU.subtract).then_inc(hs_lo, 1)
                        else:
                            dve.tensor_tensor(h_lo[:, gs], y_view(i), f32(h_hi[:, gs]), ALU.subtract).then_inc(hs_lo, 1)
                    v = due(n, "out", i)
                    if v is not None and v >= HOP2:
                        g = 2 * VISITS[v][1] + i
                        gs = slice(g * BANK, (g + 1) * BANK)
                        dve.wait_ge(y_ok, 2 * (v - LAST2 - 1) + i + 1)
                        dve.tensor_tensor(x[:, gs], y_view(i), x[:, gs], ALU.add).then_inc(o_ok, 1)

        @block.tensor
        def _(pe):
            def product(dst, w_hi, w_lo, m_hi, m_lo, first, last):
                pe.matmul(dst, w_hi, m_hi, start=first, stop=False)
                pe.matmul(dst, w_hi, m_lo, start=False, stop=False)
                return pe.matmul(dst, w_lo, m_hi, start=False, stop=last)

            half = [slice(b * BANK, (b + 1) * BANK) for b in range(2)]

            def tile_product(k, r, first, last, chunks, w_hi=h_hi, w_lo=h_lo):
                wh, wl = w_hi[:, k * P:(k + 1) * P], w_lo[:, k * P:(k + 1) * P]
                if first or last:
                    for b in range(2):
                        if first and chunks is not None:
                            pe.wait_ge(p_out, 2 * chunks - 1 + b)
                        end = product(psP[:, b, :], wh, wl, hi[:, r, half[b]], lo[:, r, half[b]], first, last)
                        if last and b == 0:
                            end.then_inc(p_half, 1)
                    return end
                return both_banks(psP, r, wh, wl, False, False)

            def both_banks(dst, r, wh, wl, first, last):
                for m in (hi, lo):
                    for b in range(2):
                        pe.matmul(dst[:, b, :], wh, m[:, r, half[b]], start=first and m is hi, stop=False)
                for b in range(2):
                    end = pe.matmul(dst[:, b, :], wl, hi[:, r, half[b]], start=False, stop=last)
                return end

            def rows(i, t):
                return pt[:, i * BANK + t * P:i * BANK + (t + 1) * P]

            def row_product(e, bank, src, w):
                for t in range(GT):
                    end = pe.matmul(psE[:, bank, t * P:(t + 1) * P], src(t), w[:, :], start=True, stop=True)
                end.then_inc(e_done, 1)

            pe.wait_ge(ident_ok, 1)

            def q_product(J, q, hj):
                I, u = q // 4, q % 4
                g = J * SLOTS + q
                pe.wait_ge(t_lo, g + 1)
                if u == 0 and not (isinstance(J, int) and J == 0 and I < 2):
                    pe.wait_ge(q_added, J * SUP + I - 1)
                for b in range(2):
                    j = 2 * u + b
                    wh, wl = hj(j)
                    bs = slice(b * BANK, (b + 1) * BANK)
                    end = product(psQ[:, I % 2, :], wh, wl, hi[:, 2 + q % 2, bs], lo[:, 2 + q % 2, bs],
                                  first=(j == 0), last=(j == TS - 1))
                end.then_inc(t_used, 1)

            def slab(J, first=False, last=False):
                if first or last:
                    hj = lambda j: (h_hi[:, (J * TS + j) * P:(J * TS + j + 1) * P], h_lo[:, (J * TS + j) * P:(J * TS + j + 1) * P])
                else:
                    hj = lambda j: (hj_hi[:, j * P:(j + 1) * P], hj_lo[:, j * P:(j + 1) * P])
                for q in range(SLOTS + LAG):
                    g = J * SLOTS + q
                    I, u = q // 4, q % 4
                    if q < SLOTS:
                        if u == 0:
                            pe.wait_ge(*nat_landed(J, q))
                            pe.wait_ge(*nat_landed(J, q + 2))
                        for b in range(2):
                            if not (first and q == 0):
                                pe.wait_ge(t_out, 2 * g + b - 1)
                            j = 2 * u + b
                            for r in range(4):
                                end = pe.transpose(psT[:, b, r * P:(r + 1) * P],
                                                   nat_tile(4 * I + r, j * P, P), ident[:, :])
                            end.then_inc(t_done, 1)
                        if first and u == 0:
                            pe.wait_ge(hs_lo, max(I + 1, 2))
                        pe.wait_ge(nat_lo, g + 1)
                        tile_product(q, q % 2, q == 0, q == SLOTS - 1,
                                     None if first else J).then_inc(nat_used, 1)
                    if q >= LAG:
                        if q == LAG and not first and not last:
                            pe.wait_ge(hj_ok, J)
                        q_product(J, q - LAG, hj)
                    if not first and q in (2, 3):
                        i = q - 2
                        pe.wait_ge(p_out, 2 * J - 1 + i)
                        row_product(2 * (J - 1) + i, i, lambda t, i=i: rows(i, t), wo)
                    if last and u == 3 and 1 <= I < SUP:
                        G = I - 1
                        e = 2 * (SL - 1) + G
                        pe.wait_ge(q_added, J * SUP + G + 1)
                        pe.wait_ge(e_used, e - 1)
                        row_product(e, G % 2, lambda t, G=G: acc[:, G * BANK + t * P:G * BANK + (t + 1) * P], wi)

            slab(0, first=True)
            pe.wait_ge(w_in_sem, 16 * 6)
            with pe.Fori(1, SL - 1) as J:
                slab(J)
            slab(SL - 1, last=True)

            def last_of_pass0(k):
                if k == 2:
                    G = NG - 1
                    pe.wait_ge(q_added, SL * SUP)
                    pe.wait_ge(e_used, 2 * SL + NG - 4)
                    row_product(2 * (SL - 1) + G, G % 2, lambda t: acc[:, G * BANK + t * P:G * BANK + (t + 1) * P], wi)
                for i in range(2):
                    if k == 4 + i:
                        pe.wait_ge(p_out, 2 * SL - 1 + i)
                        pe.wait_ge(e_used, 2 * SL + NG - 3 + i)
                        row_product(2 * SL + NG - 2 + i, i, lambda t: rows(i, t), wo)

            def last_chunk(c, k):
                for i in range(2):
                    if k == 4 + i:
                        pe.wait_ge(p_out, 2 * (SL + c) - 1 + i)
                        pe.wait_ge(e_used, E0 + 2 * (c - 1) + i - 1)
                        for t in range(GT):
                            end = pe.transpose(psE[:, i, t * P:(t + 1) * P], rows(i, t), ident[:, :])
                        end.then_inc(e_done, 1)
                    if k == 16 + 2 * i:
                        pe.wait_ge(hn_ok, LN2 + 2 * (c - 1) + i + 1)
                        for t in range(GT):
                            end = pe.transpose(psT[:, i, t * P:(t + 1) * P], rows(i, t), ident[:, :])
                        end.then_inc(ht_done, 1)
                    if k == 20 + 2 * i:
                        pe.wait_ge(ht_out, 2 * (c - 1) + i + 1)
                        for t in range(GT):
                            end = pe.matmul(psQ[:, i, t * P:(t + 1) * P], stage[:, i, 0, t * P:(t + 1) * P], w2a[:, :],
                                            start=True, stop=True)
                        end.then_inc(g_done, 1)

            def chunk(oc, lead=False, last=False):
                for k in range(T):
                    if lead and k % GT == 0:
                        pe.wait_ge(hs_lo, NG + k // GT + 1)
                    pe.wait_ge(a_lo, oc * T + k + 1)
                    tile_product(k, k % 4, k == 0, k == T - 1, SL + oc).then_inc(a_used, 1)
                    if lead:
                        last_of_pass0(k)
                    else:
                        last_chunk(oc, k)

            chunk(0, lead=True)
            with pe.Fori(1, SL - 1) as oc:
                chunk(oc)
            chunk(SL - 1, last=True)

            for n in range(len(TILES) + TAIL):
                if n < len(TILES):
                    v, k = TILES[n]
                    p, c, Js, both = VISITS[v]
                    first, last = n == END[v] - TS * len(Js), n == END[v] - 1
                    if k % GT == 0:
                        pe.wait_ge(hs_lo, split_count(p, k))
                    pe.wait_ge(a_lo, base(2) + n + 1)
                    if k // TS in both:
                        if k % GT == 0:
                            pe.wait_ge(hs_lo, split_count(p + 1, k))
                        opens = n == END[v] - TS * len(both)
                        if opens and v == BOTH[0]:
                            pe.wait_ge(g_used, 2 * SL)
                        elif opens:
                            pe.wait_ge(part_out, 2 * BOTH.index(v))
                        u_hi, u_lo = (g_hi, g_lo) if p == 2 else (h_hi, h_lo)
                        both_banks(psQ, n % 4, u_hi[:, k * P:(k + 1) * P], u_lo[:, k * P:(k + 1) * P], opens, last)
                    w_hi, w_lo = (g_hi, g_lo) if p == 3 else (h_hi, h_lo)
                    tile_product(k, n % 4, first, last, chunks_done(v) - 1, w_hi, w_lo).then_inc(a_used, 1)
                if n < T:
                    last_chunk(SL, n)
                for i in range(2):
                    v = due(n, "rows", i)
                    if v is not None:
                        pe.wait_ge(p_out, 2 * chunks_done(v) - 1 + i)
                        pe.wait_ge(e_used, e_index(v, i) - 1)
                        row_product(e_index(v, i), i, lambda t: rows(i, t), w2b if v <= LAST2 else w3)



_OUTS = [((4096, 128), "float32")]
_INS = ["x", "adj", "L0_gnn_W_in", "L0_gnn_W_out", "L2_gnn_weight", "L3_gnn_W", "L3_gnn_b"]


def kernel(**inputs):
    import numpy as _np
    import concourse.bacc as _bacc
    from concourse import mybir as _mybir
    from concourse.bass_utils import run_bass_kernel_spmd as _run

    nc = _bacc.Bacc("TRN2", target_bir_lowering=False, num_devices=1)
    arrays, args = {}, []
    for name in _INS:
        a = _np.ascontiguousarray(inputs[name])
        arrays[f"in_{name}_dram"] = a
        args.append(nc.dram_tensor(f"in_{name}_dram", a.shape, _mybir.dt.from_np(a.dtype), kind="ExternalInput").ap())
    for i, (shape, dtype) in enumerate(_OUTS):
        dt = _mybir.dt.from_np(_np.dtype(dtype))
        args.append(nc.dram_tensor(f"out_{i}_dram", shape, dt, kind="ExternalOutput").ap())
    gnn_stack_kernel(nc, *args)
    r = _run(nc, [arrays], core_ids=[0])
    return r.results[0]["out_0_dram"]
```

```python
from contextlib import ExitStack

import concourse.bass as bass
from concourse import mybir

P = 128
BANK = 512
F32 = mybir.dt.float32
F32R = mybir.dt.float32r
ALU = mybir.AluOpType
ACT = mybir.ActivationFunctionType
AX = mybir.AxisListType
FLT_MAX = 3.4028234663852886e38
EPS = 1e-5


def gnn_stack_kernel(nc, x_in, adj, w_in, w_out, w_l2, w_l3, b_l3, out):
    N, D = x_in.shape
    assert D == P and N == 4096
    T = N // P
    WIDE = 1024
    SL = N // WIDE
    TS = WIDE // P
    GT = BANK // P
    NG = T // GT
    SUP = N // BANK
    SLOTS = SUP * 4
    LAG = 2
    NRAW = 5
    RING0 = 4
    KEEP = 2
    PAIRS = (T - KEEP) // 2

    adj_t = adj.rearrange("(t p) c -> p t c", p=P)
    x_t = x_in.rearrange("(t p) d -> p t d", p=P)
    out_t = out.rearrange("(t p) d -> p t d", p=P)
    adjT = nc.dram_tensor("adjT_scratch", [SL, T, P, WIDE], F32, kind="Internal").ap()
    adjT_v = adjT.rearrange("s t p c -> p s t c")

    ctx = ExitStack()
    with ctx:
        def sb(name, shape, dt=F32):
            return ctx.enter_context(nc.sbuf_tensor(name, shape, dt))

        def sem(name):
            return ctx.enter_context(nc.semaphore(name))

        raw = sb("raw", [P, NRAW, 2, WIDE])
        hi = sb("hi", [P, 4, WIDE], F32R)
        lo = sb("lo", [P, 4, WIDE], F32R)
        stage = sb("stage", [P, 4, 2, BANK])
        h_hi = sb("h_hi", [P, T * P], F32R)
        h_lo = sb("h_lo", [P, T * P], F32R)
        KEEP_AT = nc.sbuf_base
        g_hi = sb("g_hi", [P, T * P], F32R)
        g_lo = sb("g_lo", [P, T * P], F32R)
        hj_hi = sb("hj_hi", [P, WIDE], F32R)
        hj_lo = sb("hj_lo", [P, WIDE], F32R)
        keep = nc.alloc_sbuf_tensor_at("keep", [P, KEEP, N], F32, offset=KEEP_AT)
        acc = sb("acc", [P, N])
        x = sb("x", [P, T * P])
        pt = sb("pt", [P, WIDE])
        wi = sb("wi", [P, P])
        wo = sb("wo", [P, P])
        w2a = sb("w2a", [P, P])
        w2b = sb("w2b", [P, P])
        w3 = sb("w3", [P, P])
        b3 = sb("b3", [P, P])
        ident = sb("ident", [P, P])
        rs_part = sb("rs_part", [P, SL, T])
        cs_part = sb("cs_part", [P, SL, TS * SUP])
        rs = sb("rs", [P, T])
        rs_pos = sb("rs_pos", [P, T])
        rs_den = sb("rs_den", [P, T])
        rs_inv = sb("rs_inv", [P, T])
        cs = sb("cs", [P, T])
        cs_pos = sb("cs_pos", [P, TS])
        cs_is0 = sb("cs_is0", [P, TS])
        cs_den = sb("cs_den", [P, TS])
        cs_inv = sb("cs_inv", [P, TS])
        rs_is0 = sb("rs_is0", [P, T])
        c1_raw = sb("c1_raw", [P, T])
        c1_safe = sb("c1_safe", [P, T])
        c1_ok = sb("c1_ok", [P, T])
        c1 = sb("c1", [P, T])
        stats = sb("stats", [P, 2, GT, 6])
        meanvar = sb("meanvar", [P, 2, GT, 2])
        var_eps = sb("var_eps", [P, 2, GT])
        rstd = sb("rstd", [P, 2, GT])
        minus_half = sb("minus_half", [P, GT])

        psP = ctx.enter_context(nc.psum_tensor("psP", [P, 2, BANK], F32))
        psT = ctx.enter_context(nc.psum_tensor("psT", [P, 2, BANK], F32))
        psQ = ctx.enter_context(nc.psum_tensor("psQ", [P, 2, BANK], F32))
        psE = ctx.enter_context(nc.psum_tensor("psE", [P, 2, BANK], F32))

        raw_in = [sem(f"raw_in{s}") for s in range(NRAW)]
        keep_in = sem("keep_in")
        early_in = sem("early_in")
        x_loaded = [sem(f"x_loaded{q}") for q in range(SL)]
        w_in_sem = sem("weights_loaded")
        ident_zero = sem("ident_zero")
        ident_ok = sem("ident_ok")
        nat_hi = sem("nat_hi")
        nat_lo = sem("nat_lo")
        nat_used = sem("nat_used")
        t_done = sem("t_done")
        t_out = sem("t_out")
        t_hi = sem("t_hi")
        t_hi_act = sem("t_hi_act")
        t_lo = sem("t_lo")
        t_used = sem("t_used")
        stored = [sem(f"stored{h}") for h in range(2)]
        acc_zero = sem("acc_zero")
        q_added = sem("q_added")
        hj_hi_ok = sem("hj_hi_ok")
        hj_lo_ok = sem("hj_lo_ok")
        cs_sum = sem("cs_sum")
        rs_sum = sem("rs_sum")
        cs_step = sem("cs_step")
        cs_den_ok = sem("cs_den_ok")
        cs_inv_ok = sem("cs_inv_ok")
        rs_step = sem("rs_step")
        rs_den_ok = sem("rs_den_ok")
        rs_inv_ok = sem("rs_inv_ok")
        c1_step = sem("c1_step")
        a_hi = sem("a_hi")
        a_lo = sem("a_lo")
        a_used = sem("a_used")
        p_half = sem("p_half")
        p_out = sem("p_out")
        e_done = sem("e_done")
        e_used = sem("e_used")
        ln_stats = sem("ln_stats")
        ln_mv = sem("ln_mv")
        ln_eps = sem("ln_eps")
        ln_rstd = sem("ln_rstd")
        half_ok = sem("half_ok")
        hn_ok = sem("hn_ok")
        pool_late = sem("pool_late")
        hs_hi = sem("hs_hi")
        hs_lo = sem("hs_lo")
        ht_done = sem("ht_done")
        ht_out = sem("ht_out")
        g_done = sem("g_done")
        g_out = sem("g_out")
        g_used = sem("g_used")
        part_out = sem("part_out")
        y_ok = sem("y_ok")
        o_ok = sem("o_ok")
        o_out = sem("o_out")

        def f32(ap):
            return ap.bitcast(F32)

        def cols(t, first, n):
            return t[:, bass.ds(first, n)]

        def base(p):
            return T * SL * (p - 1)

        RAW_PASS0 = [16 * SL * SUP // 2 if s < RING0 else 0 for s in range(NRAW)]
        RAW_CHUNK = PAIRS // NRAW * 16

        PLACES1 = [k % 5 if k < 20 else k % 4 for k in range(T)]

        def place2(n):
            return n % 5

        def turn1(k):
            return next(d for d in range(1, T + 1) if PLACES1[(k - d) % T] == PLACES1[k])

        def turn2(n):
            return 5 if n >= 5 else turn1(n)

        def hi_at(place):
            return hi[:, place, :] if place < 4 else hj_hi[:, :]

        def lo_at(place):
            return lo[:, place, :] if place < 4 else hj_lo[:, :]

        def slot(m):
            return (m + RING0) % NRAW

        def raw_count(kk):
            return RAW_PASS0[slot(kk)] + (kk // NRAW + 1) * 16

        def tile1(oc, k):
            if k < KEEP:
                return keep[:, k, bass.ds(oc * WIDE, WIDE)]
            return raw[:, slot((k - KEEP) // 2), k % 2, :]

        def nat_tile(r, first=0, n=WIDE):
            return raw[:, (r // 2) % RING0, r % 2, first:first + n]

        def nat_landed(J, r):
            return raw_in[(r // 2) % RING0], J * (SUP // 2 * 16) + (r // (2 * RING0) + 1) * 16

        def t_dst(q):
            return stage[:, q % 4, :, :]

        def hn_view(g):
            return acc[:, g * BANK:(g + 1) * BANK]

        def hi_on_act(q, last):
            return q % 4 != 0 if last else q % 2 == 1

        ACT_HI = SLOTS // 2
        LN0, LN1, LN2, LN3 = 0, NG, 2 * NG, 3 * NG
        E0 = 2 * SL + NG

        VISITS = [
            (2, 0, (0, 1, 2, 3), ()), (2, 1, (1, 2, 3, 0), (0,)),
            (2, 2, (2, 3, 0, 1), (0, 1)), (2, 3, (3, 0, 1, 2), (0, 1, 2)),
            (3, 2, (2, 3), ()), (3, 3, (3,), ()), (3, 1, (1, 2, 3), (2, 3)), (3, 0, (0, 2, 3, 1), (1, 2, 3)),
            (4, 3, (3, 2, 1, 0), ()), (4, 2, (3, 2, 1, 0), ()), (4, 1, (1, 0), ()), (4, 0, (0,), ())]
        TILES = [(v, J * TS + j) for v, visit in enumerate(VISITS) for J in visit[2] for j in range(TS)]
        END = [sum(TS * len(visit[2]) for visit in VISITS[:v + 1]) for v in range(len(VISITS))]
        LAST2 = 3
        HOP2 = 8
        TAIL = 19
        EARLY_BLOCKS = VISITS[HOP2 - 1][2][:3]
        EARLY = 1 + len(EARLY_BLOCKS)
        EARLY_PAIR = END[HOP2] // 2 - EARLY
        BOTH = [v for v, visit in enumerate(VISITS) if visit[3]]
        PARTS = [v for v, (p, c, Js, both) in enumerate(VISITS) if len(Js) < SL]
        AFTER0 = dict(rows=(4, 5), add=(7, 10), stats=(9, 12), aggregate=(11, 14), split=(20, 24))
        AFTER1 = dict(rows=(4, 5), add=(7, 9), stats=(11, 13), aggregate=(14, 16), turn=(20, 23),
                      turn_out=(24, 27), w_top=(25, 28), w_top_out=(29, 31))
        LAST1 = dict(AFTER1, stats=(10, 13), aggregate=(12, 15), split=(20, 26))
        STEPS2 = dict(copy=(2, 2), part=(4, 4), rows=(4, 5), add=(6, 8), stats=(10, 12), aggregate=(13, 15),
                      split=(19, 22))
        STEPS3 = dict(copy=(2, 2), part=(4, 4), rows=(4, 5), add=(6, 7),
                      split=(12, 14), silu=(8, 10), out=(12, 14), store=(16, 18))
        SOONER = dict(STEPS2, rows=(1, 2), add=(3, 4), stats=(4, 6), aggregate=(5, 8), norm=(7, 10),
                      split=(8, 12))

        def due(n, step, i):
            for v in range(len(VISITS)):
                steps = STEPS2 if v < LAST2 else SOONER if v == LAST2 else STEPS3
                if step in steps and n == END[v] + steps[step][i]:
                    return v
            return None

        def split_count(p, k):
            if p == 2:
                return NG * 2 + k // GT + 1
            made = [c for q, c, Js, both in VISITS if q == p - 1].index(k // TS)
            return NG * p + 2 * made + k % TS // GT + 1

        def is_early(m):
            return EARLY_PAIR <= m < EARLY_PAIR + EARLY

        def ring_pair(m):
            return m if m < EARLY_PAIR else m - EARLY

        def pair_landed(m):
            if is_early(m):
                return early_in, 16 * (m - EARLY_PAIR + 1)
            return raw_in[slot(ring_pair(m))], SL * RAW_CHUNK + raw_count(ring_pair(m))

        def pair_place(m):
            if is_early(m):
                if m == EARLY_PAIR:
                    return acc[:, 2 * WIDE:4 * WIDE].rearrange("p (t c) -> p t c", c=WIDE)
                J = EARLY_BLOCKS[m - EARLY_PAIR - 1]
                return keep[:, :, J * WIDE:(J + 1) * WIDE]
            return raw[:, slot(ring_pair(m)), :, :]

        def tile2(n):
            return pair_place(n // 2)[:, n % 2, :]

        def product_of(v):
            return psP if v % 2 == 0 else psT

        def chunks_done(v):
            return 2 * SL + v + 1

        def e_index(v, i):
            return E0 + 2 * (SL + v) + i

        def y_view(i):
            return stage[:, 2 + i, 0, :]

        def z_view(i):
            return stage[:, i, 1, :]

        def norm_view(i):
            return stage[:, i, 0, :]

        block = ctx.enter_context(nc.Block())

        @block.sync
        def _(sp):
            def load_super(J, I, guard):
                for half in range(2):
                    s = (2 * I + half) % RING0
                    if guard and half == 0:
                        sp.wait_ge(nat_used, J * SLOTS + I * 4 - 4)
                    sp.dma_start(raw[:, s, :, :],
                                 adj_t[:, 4 * I + 2 * half:4 * I + 2 * half + 2, bass.ds(J * WIDE, WIDE)]
                                 ).then_inc(raw_in[s], 16)

            def store_half(J, I, h):
                sp.wait_ge(t_out, (J * SLOTS + 4 * I + 2 * h + 2) * 2)
                src = stage[:, 2 * h:2 * h + 2, :, :].rearrange("p u b c -> p (u b) c")
                sp.dma_start(adjT_v[:, I // 2, bass.ds(J * TS + 4 * h, 4), (I % 2) * BANK:(I % 2 + 1) * BANK],
                             src).then_inc(stored[h], 16)

            def load_pair(oc, kk):
                sp.dma_start(raw[:, slot(kk), :, :], adj_t[:, KEEP + 2 * kk:KEEP + 2 * kk + 2, bass.ds(oc * WIDE, WIDE)]
                             ).then_inc(raw_in[slot(kk)], 16)

            def slab(J, first=False, last=False):
                for I in range(SUP):
                    if I + 1 < SUP:
                        load_super(J, I + 1, guard=not (first and I == 0))
                    elif not last:
                        load_super(J + 1, 0, guard=True)
                    if last and 1 <= I <= SL:
                        sp.dma_start(keep[:, :, (I - 1) * WIDE:I * WIDE],
                                     adj_t[:, 0:KEEP, (I - 1) * WIDE:I * WIDE]).then_inc(keep_in, 16)
                    if last and I == SUP - 2:
                        load_pair(0, 0)
                    if last and I == SUP - 1:
                        sp.wait_ge(nat_used, SL * SLOTS - 4)
                        load_pair(0, 1)
                        load_pair(0, 2)
                    store_half(J, I, 0)
                    store_half(J, I, 1)

            sp.dma_start(x[:, 0:BANK].rearrange("p (t d) -> p t d", d=P), x_t[:, 0:GT, :]).then_inc(x_loaded[0], 16)
            sp.dma_start(x[:, BANK:WIDE].rearrange("p (t d) -> p t d", d=P), x_t[:, GT:TS, :]).then_inc(x_loaded[1], 16)
            load_super(0, 0, guard=False)
            sp.dma_start(x[:, WIDE:2 * WIDE].rearrange("p (t d) -> p t d", d=P), x_t[:, TS:2 * TS, :]).then_inc(x_loaded[2], 16)
            sp.dma_start(x[:, 2 * WIDE:].rearrange("p (t d) -> p t d", d=P), x_t[:, 2 * TS:, :]).then_inc(x_loaded[3], 16)
            for w, src in ((wi, w_in), (wo, w_out), (w2a, w_l2[0:P, :]), (w2b, w_l2[P:2 * P, :]), (w3, w_l3)):
                sp.dma_start(w[:, :], src).then_inc(w_in_sem, 16)
            sp.dma_start(b3[:, :], b_l3.partition_broadcast(P)).then_inc(w_in_sem, 16)
            slab(0, first=True)
            with sp.Fori(1, SL - 1) as J:
                slab(J)
            slab(SL - 1, last=True)

            def load_chunk(oc, lead):
                for kk in range(PAIRS):
                    if lead and kk < 3:
                        continue
                    if lead and kk < NRAW:
                        if kk == 3:
                            sp.wait_ge(nat_used, SL * SLOTS)
                    elif kk >= NRAW:
                        sp.wait_ge(a_lo, oc * T + KEEP + 2 * (kk - NRAW) + 2)
                    else:
                        sp.wait_ge(a_lo, oc * T - T + KEEP + 2 * (kk + PAIRS - NRAW) + 2)
                    load_pair(oc, kk)

            load_chunk(0, True)
            with sp.Fori(1, SL) as oc:
                load_chunk(oc, False)

            for h in range(2):
                sp.wait_ge(stored[h], 16 * SL * SUP)
            def load_visit_pair(m):
                v, k = TILES[2 * m]
                place = pair_place(m)
                sp.dma_start(place, adjT_v[:, VISITS[v][1], k:k + 2, :]).then_inc(pair_landed(m)[0], 16)

            for m in range(len(TILES) // 2):
                if is_early(m):
                    continue
                r = ring_pair(m)
                if r >= NRAW:
                    freed = 2 * (r - NRAW) + 2 + (2 * EARLY if r - NRAW >= EARLY_PAIR else 0)
                else:
                    freed = KEEP - T + 2 * (r + PAIRS - NRAW) + 2
                for e in range(EARLY):
                    if freed - END[HOP2 - 2] == TS * e + 4:
                        if e == 0:
                            sp.wait_ge(p_out, 2 * chunks_done(HOP2 - 3))
                        else:
                            sp.wait_ge(a_used, base(2) + END[HOP2 - 2] + TS * e)
                        load_visit_pair(EARLY_PAIR + e)
                sp.wait_ge(a_lo, base(2) + freed)
                load_visit_pair(m)

        @block.gpsimd
        def _(pool):
            pool.memset(ident[:, :], 0.0).then_inc(ident_zero, 1)
            pool.wait_ge(ident_zero, 1)
            pool.affine_select(out=ident[:, :], in_=ident[:, :], compare_op=ALU.not_equal, fill=1.0,
                               base=0, pattern=[[-1, P]], channel_multiplier=1).then_inc(ident_ok, 1)

            pool.memset(minus_half[:, :], -0.5).then_inc(half_ok, 1)
            pool.wait_ge(half_ok, 1)

            def norm_factors(i, index):
                pool.wait_ge(ln_mv, index + 1)
                pool.tensor_scalar(var_eps[:, i, :], meanvar[:, i, :, 1], EPS, None, op0=ALU.add).then_inc(ln_eps, 1)
                pool.wait_ge(ln_eps, index + 1)
                pool.tensor_tensor(rstd[:, i, :], var_eps[:, i, :], minus_half[:, :], ALU.pow).then_inc(ln_rstd, 1)

            def normalise(i, index, first_col, dst, first_dst):
                norm_factors(i, index)
                pool.wait_ge(ln_rstd, index + 1)
                for t in range(GT):
                    ins = pool.tensor_scalar(dst[:, first_dst + t * P:first_dst + (t + 1) * P],
                                             x[:, first_col + t * P:first_col + (t + 1) * P],
                                             meanvar[:, i, t, 0:1], rstd[:, i, t:t + 1],
                                             op0=ALU.subtract, op1=ALU.mult)
                ins.then_inc(hn_ok, 1)

            def slab(J):
                pool.wait_ge(cs_sum, J + 1)
                pool.tensor_scalar(cs_pos[:, :], cols(cs, J * TS, TS), 0.0, None, op0=ALU.max).then_inc(cs_step, 1)
                pool.tensor_scalar(cs_is0[:, :], cols(cs, J * TS, TS), 0.0, None, op0=ALU.is_le).then_inc(cs_step, 1)
                pool.wait_ge(cs_step, 2 * (J + 1))
                if J > 0:
                    pool.wait_ge(cs_inv_ok, J)
                pool.tensor_tensor(cs_den[:, :], cs_pos[:, :], cs_is0[:, :], ALU.add).then_inc(cs_den_ok, 1)

            for g in range(NG):
                norm_factors(g % 2, LN0 + g)
            for J in range(1, SL):
                if J < SL - 1:
                    if J == 1:
                        pool.wait_ge(hs_lo, NG)
                    else:
                        pool.wait_ge(t_used, J * SLOTS)
                    pool.tensor_copy(hj_hi[:, :], f32(cols(h_hi, J * WIDE, WIDE))).then_inc(hj_hi_ok, 1)
                slab(J - 1)
            for I in range(SUP):
                if I >= 2:
                    G = I - 2
                    normalise(G % 2, LN1 + G, G * BANK, acc, G * BANK)
                r = slice(GT * I, GT * I + GT)
                pool.wait_ge(rs_sum, I + 1)
                pool.tensor_scalar(rs_pos[:, r], rs[:, r], 0.0, None, op0=ALU.max).then_inc(rs_step, 1)
                pool.tensor_scalar(rs_is0[:, r], rs[:, r], 0.0, None, op0=ALU.is_le).then_inc(rs_step, 1)
                pool.wait_ge(rs_step, 2 * I + 2)
                pool.tensor_tensor(rs_den[:, r], rs_pos[:, r], rs_is0[:, r], ALU.add).then_inc(rs_den_ok, 1)
            slab(SL - 1)
            for G in range(NG - 2, NG):
                normalise(G % 2, LN1 + G, G * BANK, acc, G * BANK)
            pool.wait_ge(c1_step, 3)
            pool.tensor_tensor(c1[:, :], c1_safe[:, :], c1_ok[:, :], ALU.mult).then_inc(pool_late, 1)

            for c in range(SL):
                for i in range(2):
                    normalise(i, LN2 + 2 * c + i, c * WIDE + i * BANK, pt, i * BANK)
                    n = 2 * c + i
                    pool.wait_ge(hn_ok, LN2 + n + 1)
                    pool.tensor_copy(acc[:, n * BANK:(n + 1) * BANK], pt[:, i * BANK:(i + 1) * BANK]).then_inc(pool_late, 1)
                for i in range(2):
                    xg = x[:, c * WIDE + i * BANK:c * WIDE + (i + 1) * BANK]
                    pool.wait_ge(g_out, 2 * c + i + 1)
                    pool.tensor_tensor(xg, z_view(i), xg, ALU.add).then_inc(g_used, 1)
            stage_cols = stage[:, :, :, :].rearrange("p u b c -> p (u b c)")
            for v in range(LAST2 + 1):
                for i in range(2):
                    if v < LAST2:
                        normalise(i, LN3 + 2 * v + i, VISITS[v][1] * WIDE + i * BANK, stage_cols, 2 * i * BANK)
                    else:
                        norm_factors(i, LN3 + 2 * v + i)

        @block.scalar
        def _(act):
            def split_h(g, src, index, func):
                if index >= LN2:
                    act.wait_ge(pool_late, 1 + g + 1)
                else:
                    act.wait_ge(hn_ok, index + 1)
                act.activation(h_hi[:, g * BANK:(g + 1) * BANK], src, func).then_inc(hs_hi, 1)

            def split_group(p, g):
                split_h(g, hn_view(g), NG * p + g, ACT.Relu)

            def natural_hi(J, q, first):
                g = J * SLOTS + q
                if q % 2 == 0:
                    act.wait_ge(*nat_landed(J, q))
                if not (first and q < 2):
                    act.wait_ge(nat_used, g - 1)
                act.activation(hi[:, q % 2, :], nat_tile(q), ACT.Copy,
                               accum_out=rs_part[:, bass.ds(J, 1), q:q + 1].rearrange("p a b -> p (a b)")).then_inc(nat_hi, 1)

            def slab(J, first=False, last=False):
                natural_hi(J, 0, first)
                if first:
                    split_h(1, pt[:, BANK:2 * BANK], LN0 + 1, ACT.Relu)
                if not first:
                    for b in range(2):
                        if b == 0:
                            act.wait_ge(p_half, J)
                        else:
                            act.wait_ge(nat_used, J * SLOTS)
                        act.activation(pt[:, b * BANK:(b + 1) * BANK], psP[:, b, :], ACT.Copy).then_inc(p_out, 1)
                for q in range(SLOTS):
                    g = J * SLOTS + q
                    u = q % 4
                    if q + 1 < SLOTS:
                        natural_hi(J, q + 1, first)
                    if not (first and q < 4):
                        act.wait_ge(stored[u // 2], 16 * (J * SUP + q // 4))
                        act.wait_ge(t_lo, g - 3)
                    for b in range(2):
                        act.wait_ge(t_done, 2 * g + b + 1)
                        act.activation(t_dst(q)[:, b, :], psT[:, b, :], ACT.Copy,
                                       accum_out=cs_part[:, bass.ds(J, 1), (2 * u + b) * SUP + q // 4:(2 * u + b) * SUP + q // 4 + 1]
                                       .rearrange("p a b -> p (a b)")).then_inc(t_out, 1)
                    if hi_on_act(q, last):
                        act.wait_ge(t_out, 2 * g + 2)
                        if not (first and q < 2):
                            act.wait_ge(t_used, g - 1)
                        act.activation(hi[:, 2 + q % 2, :].rearrange("p (b c) -> p b c", b=2), t_dst(q),
                                       ACT.Copy).then_inc(t_hi_act, 1)
                    if q == 0 and not first and not last:
                        act.wait_ge(t_used, J * SLOTS)
                        act.activation(hj_lo[:, :], f32(cols(h_lo, J * WIDE, WIDE)), ACT.Copy).then_inc(hj_lo_ok, 1)
                    if last and u == 3 and q // 4 >= 3:
                        split_group(1, q // 4 - 3)
                    if first and q % 4 == 1 and 1 <= q // 4 <= NG - 2:
                        n = q // 4 + 1
                        split_h(n, pt[:, n % 2 * BANK:(n % 2 + 1) * BANK], LN0 + n, ACT.Relu)

            split_h(0, pt[:, 0:BANK], LN0, ACT.Relu)
            slab(0, first=True)
            with act.Fori(1, SL - 1) as J:
                slab(J)
            slab(SL - 1, last=True)

            def copy_product(src, count, ready):
                for b in range(2):
                    if b == 0:
                        act.wait_ge(p_half, count)
                    else:
                        act.wait_ge(*ready)
                    act.activation(pt[:, b * BANK:(b + 1) * BANK], src[:, b, :], ACT.Copy).then_inc(p_out, 1)

            def lead_splits(p, k):
                if p == 2 and k == 3:
                    split_group(p, NG - 4)
                if k == 5:
                    split_group(p, NG - 3)
                for i in range(2):
                    if k == (AFTER0 if p == 1 else LAST1)["split"][i]:
                        split_group(p, NG - 2 + i)

            def transposed_norms(c, k):
                for i in range(2):
                    if k == AFTER1["turn_out"][i]:
                        act.wait_ge(ht_done, 2 * (c - 1) + i + 1)
                        act.activation(norm_view(i), psT[:, i, :], ACT.Relu).then_inc(ht_out, 1)
                    if k == AFTER1["w_top_out"][i]:
                        act.wait_ge(g_done, 2 * (c - 1) + i + 1)
                        act.activation(z_view(i), psQ[:, i, :], ACT.Copy).then_inc(g_out, 1)

            def chunk(oc, lead=False, last=False):
                for k in range(T):
                    n = oc * T + k
                    if k % 2 == 0 and k >= KEEP:
                        kk = (k - KEEP) // 2
                        act.wait_ge(raw_in[slot(kk)], oc * RAW_CHUNK + raw_count(kk))
                    if lead and k == 0:
                        act.wait_ge(keep_in, 16 * SL)
                    if lead and k < 4:
                        if k == 0:
                            act.wait_ge(nat_used, SL * SLOTS)
                        if k == 2:
                            act.wait_ge(t_used, SL * SLOTS)
                    elif not (lead and k == 4):
                        act.wait_ge(a_used, n - turn1(k) + 1)
                    act.activation(hi_at(PLACES1[k]), tile1(oc, k), ACT.Copy).then_inc(a_hi, 1)
                    if k == 1:
                        if lead:
                            copy_product(psP, SL, (nat_used, SL * SLOTS))
                        else:
                            act.wait_ge(pool_late, 2 * oc - 1)
                            copy_product(psP, SL + oc, (a_used, oc * T))
                    if lead:
                        lead_splits(1, k)
                    else:
                        transposed_norms(oc, k)
                    if last and k % GT == 3 and 2 <= k // GT < NG - 2:
                        split_group(2, k // GT - 2)
                if lead:
                    for h in range(2):
                        act.wait_ge(stored[h], 16 * SL * SUP)

            chunk(0, lead=True)
            with act.Fori(1, SL - 1) as oc:
                chunk(oc)
            chunk(SL - 1, last=True)

            for n in range(len(TILES) + TAIL):
                if n < len(TILES):
                    if n % 2 == 0:
                        act.wait_ge(*pair_landed(n // 2))
                    act.wait_ge(a_used, base(2) + n - turn2(n) + 1)
                    act.activation(hi_at(place2(n)), tile2(n), ACT.Copy).then_inc(a_hi, 1)
                if n < T:
                    if n == 1:
                        act.wait_ge(pool_late, 2 * SL - 1)
                        copy_product(psP, 2 * SL, (a_used, base(2)))
                    lead_splits(2, n)
                    transposed_norms(SL, n)
                v = due(n, "copy", 0)
                if v is not None:
                    if v not in PARTS:
                        copy_product(product_of(v), chunks_done(v), (a_used, base(2) + END[v]))
                v = due(n, "part", 0)
                if v is not None:
                    if v in BOTH:
                        c = VISITS[v][1]
                        if v in PARTS:
                            act.wait_ge(p_out, 2 * chunks_done(v))
                        if v == BOTH[0]:
                            act.wait_ge(hs_lo, 3 * NG)
                        act.wait_ge(a_used, base(2) + END[v])
                        for b in range(2):
                            act.activation(acc[:, c * WIDE + b * BANK:c * WIDE + (b + 1) * BANK], psQ[:, b, :],
                                           ACT.Copy).then_inc(part_out, 1)
                for i in range(2):
                    v = due(n, "silu", i)
                    if v is not None:
                        act.wait_ge(e_used, e_index(v, i) + 1)
                        act.activation(y_view(i), z_view(i), ACT.Silu).then_inc(y_ok, 1)
                    v = due(n, "split", i)
                    if v is not None and v < HOP2:
                        g = 2 * VISITS[v][1] + i
                        gs = slice(g * BANK, (g + 1) * BANK)
                        if v <= LAST2:
                            act.wait_ge(hn_ok, LN3 + 2 * v + i + 1)
                            act.activation(g_hi[:, gs], norm_view(i), ACT.Relu).then_inc(hs_hi, 1)
                        else:
                            act.wait_ge(y_ok, 2 * (v - LAST2 - 1) + i + 1)
                            act.activation(h_hi[:, gs], y_view(i), ACT.Copy).then_inc(hs_hi, 1)
                    v = due(n, "store", i)
                    if v is not None and v >= HOP2:
                        g = 2 * VISITS[v][1] + i
                        act.wait_ge(o_ok, 2 * (v - HOP2) + i + 1)
                        act.dma_start(out_t[:, g * GT:(g + 1) * GT, :],
                                      x[:, g * BANK:(g + 1) * BANK].rearrange("p (t d) -> p t d", d=P)).then_inc(o_out, 16)
            act.wait_ge(o_out, 16 * NG)

        @block.vector
        def _(dve):
            def ln_a(i, rows):
                for t in range(GT):
                    ins = dve.bn_stats(stats[:, i, t, :], rows(t))
                ins.then_inc(ln_stats, 1)

            def ln_b(i):
                for t in range(GT):
                    ins = dve.bn_aggr(meanvar[:, i, t, :], stats[:, i, t, :])
                ins.then_inc(ln_mv, 1)

            def ln_d(i, index, rows, dst):
                dve.wait_ge(ln_rstd, index + 1)
                for t in range(GT):
                    ins = dve.tensor_scalar(dst(t), rows(t), meanvar[:, i, t, 0:1], rstd[:, i, t:t + 1],
                                            op0=ALU.subtract, op1=ALU.mult)
                ins.then_inc(hn_ok, 1)

            def split_h(g, src, index, relu):
                dve.wait_ge(hs_hi, index + 1)
                gs = slice(g * BANK, (g + 1) * BANK)
                if relu:
                    dve.scalar_tensor_tensor(h_lo[:, gs], src, 0.0, f32(h_hi[:, gs]), op0=ALU.max, op1=ALU.subtract).then_inc(hs_lo, 1)
                else:
                    dve.tensor_tensor(h_lo[:, gs], src, f32(h_hi[:, gs]), ALU.subtract).then_inc(hs_lo, 1)

            def split_group(p, g):
                split_h(g, hn_view(g), NG * p + g, True)

            def x_rows(first_col):
                return lambda t: cols(x, first_col + t * P, P) if not isinstance(first_col, int) \
                    else x[:, first_col + t * P:first_col + (t + 1) * P]

            def scaled_add(e, bank, first_col, inv):
                dve.wait_ge(e_done, e + 1)
                xr = x_rows(first_col)
                for t in range(GT):
                    ins = dve.scalar_tensor_tensor(xr(t), psE[:, bank, t * P:(t + 1) * P], inv(t), xr(t),
                                                   op0=ALU.mult, op1=ALU.add)
                ins.then_inc(e_used, 1)

            def first_rows(g):
                return x_rows(g * BANK)

            def first_hn(g):
                return lambda t: pt[:, (g % 2) * BANK + t * P:(g % 2) * BANK + (t + 1) * P]

            def first_step(g, step):
                i = g % 2
                if step == 0:
                    dve.wait_ge(x_loaded[min(g, 2) if g < 4 else 3], 16)
                    ln_a(i, first_rows(g))
                if step == 1:
                    dve.wait_ge(ln_stats, g + 1)
                    ln_b(i)
                if step == 3:
                    if g >= 2:
                        dve.wait_ge(hs_lo, g - 1)
                    ln_d(i, g, first_rows(g), first_hn(g))

            def natural_lo(J, q):
                g = J * SLOTS + q
                dve.wait_ge(nat_hi, g + 1)
                dve.tensor_tensor(lo[:, q % 2, :], nat_tile(q), f32(hi[:, q % 2, :]), ALU.subtract).then_inc(nat_lo, 1)

            def add_q(J, I, first):
                dve.wait_ge(t_used, J * SLOTS + 4 * I + 4)
                a = acc[:, I * BANK:(I + 1) * BANK]
                if first and I < SUP - 1:
                    dve.tensor_copy(a, psQ[:, I % 2, :]).then_inc(q_added, 1)
                else:
                    if I == SUP - 1:
                        dve.wait_ge(acc_zero, 1)
                    dve.wait_ge(q_added, J * SUP + I + 1 - SUP if I < SUP - 1 else J * SUP + I)
                    dve.tensor_tensor(a, psQ[:, I % 2, :], a, ALU.add).then_inc(q_added, 1)

            def slab(J, first=False, last=False):
                natural_lo(J, 0)
                if first:
                    split_h(1, pt[:, BANK:2 * BANK], LN0 + 1, True)
                for q in range(SLOTS):
                    g = J * SLOTS + q
                    I, u = q // 4, q % 4
                    ring_t = 2 + q % 2
                    if q + 1 < SLOTS:
                        natural_lo(J, q + 1)
                    by_act = hi_on_act(q, last)
                    if not by_act:
                        dve.wait_ge(t_out, 2 * g + 2)
                        if not (first and q < 2):
                            dve.wait_ge(t_used, g - 1)
                    hi_t = hi[:, ring_t, :].rearrange("p (b c) -> p b c", b=2)
                    lo_t = lo[:, ring_t, :].rearrange("p (b c) -> p b c", b=2)
                    if not by_act:
                        dve.tensor_copy(hi_t, t_dst(q)).then_inc(t_hi, 1)
                    if u == 2 and I >= 1:
                        add_q(J, I - 1, first)
                    if first and I + 2 < NG:
                        first_step(I + 2, u)
                    if first and u == 2 and 1 <= I <= NG - 2:
                        n = I + 1
                        split_h(n, pt[:, n % 2 * BANK:(n % 2 + 1) * BANK], LN0 + n, True)
                    if not first:
                        if q == 1:
                            add_q(J - 1, SUP - 1, False)
                            dve.wait_ge(cs_den_ok, J)
                            dve.reciprocal(cs_inv[:, :], cs_den[:, :]).then_inc(cs_inv_ok, 1)
                        if q in (4, 5):
                            i = q - 4
                            if i == 0:
                                dve.wait_ge(cs_inv_ok, J)
                            scaled_add(2 * (J - 1) + i, i, J * WIDE - WIDE + i * BANK,
                                       lambda t, i=i: cs_inv[:, i * GT + t:i * GT + t + 1])
                    n_act = J * ACT_HI + sum(hi_on_act(r, last) for r in range(q + 1))
                    n_dve = J * (SLOTS - ACT_HI) + sum(not hi_on_act(r, last) for r in range(q + 1))
                    if by_act:
                        dve.wait_ge(t_hi_act, n_act)
                    else:
                        dve.wait_ge(t_hi, n_dve)
                    dve.tensor_tensor(lo_t, t_dst(q), f32(hi_t), ALU.subtract).then_inc(t_lo, 1)
                    if last and u == 3 and I >= 3:
                        split_group(1, I - 3)
                    if last:
                        if u == 0 and I >= 2:
                            row_update(I - 2)
                        if u >= 1 and I >= 2:
                            ln_group(I - 2, u - 1)
                        if u == 2 and I >= 1:
                            row_factors(I - 1)
                        if u == 3:
                            dve.wait_ge(nat_hi, J * SLOTS + q + 1)
                            part = rs_part[:, :, GT * I:GT * I + GT].rearrange("p s t -> p t s")
                            dve.reduce_sum(rs[:, GT * I:GT * I + GT], part, axis=AX.X).then_inc(rs_sum, 1)
                dve.wait_ge(t_out, J * (2 * SLOTS) + 2 * SLOTS)
                part = cs_part[:, bass.ds(J, 1), :].rearrange("p a (t s) -> p (a t) s", s=SUP)
                dve.reduce_sum(cols(cs, J * TS, TS), part, axis=AX.X).then_inc(cs_sum, 1)

            def row_factors(G):
                dve.wait_ge(rs_den_ok, G + 1)
                r = slice(G * GT, (G + 1) * GT)
                dve.reciprocal(rs_inv[:, r], rs_den[:, r]).then_inc(rs_inv_ok, 1)

            def row_update(G):
                dve.wait_ge(rs_inv_ok, G + 1)
                scaled_add(2 * (SL - 1) + G, G % 2, G * BANK,
                           lambda t: rs_inv[:, G * GT + t:G * GT + t + 1])

            def ln_group(G, step):
                if step == 0:
                    dve.wait_ge(e_used, 2 * (SL - 1) + G + 1)
                    ln_a(G % 2, x_rows(G * BANK))
                if step == 1:
                    dve.wait_ge(ln_stats, LN1 + G + 1)
                    dve.wait_ge(hn_ok, LN1 + G - 1)
                    ln_b(G % 2)

            dve.memset(acc[:, N - BANK:], 0.0).then_inc(acc_zero, 1)
            for g, step in ((0, 0), (0, 1), (1, 0), (1, 1), (0, 3), (1, 3)):
                first_step(g, step)
            split_h(0, pt[:, 0:BANK], LN0, True)
            slab(0, first=True)
            with dve.Fori(1, SL - 1) as J:
                slab(J)
            slab(SL - 1, last=True)

            def last_of_pass0(k):
                if k == 0:
                    add_q(SL - 1, SUP - 1, False)
                    row_factors(NG - 1)
                if k == 2:
                    dve.wait_ge(cs_den_ok, SL)
                    dve.reciprocal(cs_inv[:, :], cs_den[:, :]).then_inc(cs_inv_ok, 1)
                    dve.wait_ge(cs_sum, SL)
                    dve.reciprocal(c1_raw[:, :], cs[:, :]).then_inc(c1_step, 1)
                for i in range(2):
                    if k == 4 + 2 * i:
                        row_update(NG - 2 + i)
                    col = N - WIDE + i * BANK
                    if k == AFTER0["add"][i]:
                        if i == 0:
                            dve.wait_ge(cs_inv_ok, SL)
                            dve.wait_ge(e_used, 2 * (SL - 1) + NG)
                        scaled_add(2 * SL + NG - 2 + i, i, col, lambda t: cs_inv[:, i * GT + t:i * GT + t + 1])
                    if k == AFTER0["stats"][i]:
                        ln_a(i, x_rows(col))
                    if k == AFTER0["aggregate"][i]:
                        ln_b(i)
                if k == 22:
                    dve.wait_ge(c1_step, 1)
                    dve.tensor_scalar(c1_safe[:, :], c1_raw[:, :], FLT_MAX, -FLT_MAX, op0=ALU.min, op1=ALU.max).then_inc(c1_step, 1)
                if k == 24:
                    dve.wait_ge(c1_step, 2)
                    dve.tensor_tensor(c1_ok[:, :], c1_safe[:, :], c1_raw[:, :], ALU.is_equal).then_inc(c1_step, 1)

            def last_chunk(c, k, plan):
                for i in range(2):
                    col = (c - 1) * WIDE + i * BANK
                    if k == plan["add"][i]:
                        if i == 0:
                            dve.wait_ge(pool_late, 1)
                        scaled_add(E0 + 2 * (c - 1) + i, i, col, lambda t: cols(c1, (c - 1) * TS + i * GT + t, 1))
                    if k == plan["stats"][i]:
                        ln_a(i, x_rows(col))
                    if k == plan["aggregate"][i]:
                        ln_b(i)

            def norm_waits(e, ln, k, plan):
                for i in range(2):
                    if k == plan["stats"][i]:
                        dve.wait_ge(e_used, e + i + 1)
                    if k == plan["aggregate"][i]:
                        dve.wait_ge(ln_stats, ln + i + 1)

            def lead_splits(p, k):
                if p == 2 and k == 3:
                    split_group(p, NG - 4)
                if k == 5:
                    split_group(p, NG - 3)
                for i in range(2):
                    if k == (AFTER0 if p == 1 else LAST1)["split"][i]:
                        split_group(p, NG - 2 + i)

            def chunk(oc, lead=False, last=False):
                for k in range(T):
                    if lead:
                        norm_waits(2 * SL + NG - 2, LN1 + NG - 2, k, AFTER0)
                    else:
                        norm_waits(E0 + 2 * (oc - 1), LN2 + 2 * (oc - 1), k, AFTER1)
                    dve.wait_ge(a_hi, oc * T + k + 1)
                    dve.tensor_tensor(lo_at(PLACES1[k]), tile1(oc, k), f32(hi_at(PLACES1[k])),
                                      ALU.subtract).then_inc(a_lo, 1)
                    if lead:
                        lead_splits(1, k)
                        last_of_pass0(k)
                    else:
                        last_chunk(oc, k, AFTER1)
                    if last and k % GT == 3 and 2 <= k // GT < NG - 2:
                        split_group(2, k // GT - 2)

            chunk(0, lead=True)
            with dve.Fori(1, SL - 1) as oc:
                chunk(oc)
            chunk(SL - 1, last=True)

            for n in range(len(TILES) + TAIL):
                if n < T:
                    norm_waits(E0 + 2 * (SL - 1), LN2 + 2 * (SL - 1), n, LAST1)
                for i in range(2):
                    v = due(n, "stats", i)
                    if v is not None:
                        dve.wait_ge(e_used, e_index(v, i) + 1)
                    v = due(n, "aggregate", i)
                    if v is not None:
                        dve.wait_ge(ln_stats, LN3 + 2 * v + i + 1)
                if n < len(TILES):
                    dve.wait_ge(a_hi, base(2) + n + 1)
                    dve.tensor_tensor(lo_at(place2(n)), tile2(n), f32(hi_at(place2(n))),
                                      ALU.subtract).then_inc(a_lo, 1)
                if n < T:
                    lead_splits(2, n)
                    last_chunk(SL, n, LAST1)
                v = due(n, "copy", 0)
                if v is not None and v in PARTS:
                    c = VISITS[v][1]
                    dve.wait_ge(part_out, 2 * (BOTH.index(max(w for w in BOTH if VISITS[w][1] == c and w < v)) + 1))
                    for b in range(2):
                        if b == 0:
                            dve.wait_ge(p_half, chunks_done(v))
                        else:
                            dve.wait_ge(a_used, base(2) + END[v])
                        bs = slice(b * BANK, (b + 1) * BANK)
                        dve.tensor_tensor(pt[:, bs], product_of(v)[:, b, :], acc[:, c * WIDE + b * BANK:c * WIDE + (b + 1) * BANK],
                                          ALU.add).then_inc(p_out, 1)
                for i in range(2):
                    v = due(n, "add", i)
                    if v is not None:
                        col = VISITS[v][1] * WIDE + i * BANK
                        dve.wait_ge(e_done, e_index(v, i) + 1)
                        if v <= LAST2:
                            dve.wait_ge(g_used, 2 * SL)
                            dve.tensor_tensor(x[:, col:col + BANK], psE[:, i, :], x[:, col:col + BANK], ALU.add).then_inc(e_used, 1)
                        else:
                            z = z_view(i).rearrange("p (t d) -> p t d", d=P)
                            row = psE[:, i, :].rearrange("p (t d) -> p t d", d=P)
                            dve.tensor_tensor(z, row, b3[:, :].unsqueeze(1).broadcast_to([P, GT, P]), ALU.add).then_inc(e_used, 1)
                    v = due(n, "stats", i)
                    if v is not None:
                        ln_a(i, x_rows(VISITS[v][1] * WIDE + i * BANK))
                    v = due(n, "aggregate", i)
                    if v is not None:
                        ln_b(i)
                    if due(n, "norm", i) is not None:
                        ln_d(i, LN3 + 2 * LAST2 + i, x_rows(VISITS[LAST2][1] * WIDE + i * BANK),
                             lambda t: stage[:, i, 0, t * P:(t + 1) * P])
                    v = due(n, "split", i)
                    if v is not None and v < HOP2:
                        dve.wait_ge(hs_hi, 3 * NG + 2 * v + i + 1)
                        g = 2 * VISITS[v][1] + i
                        gs = slice(g * BANK, (g + 1) * BANK)
                        if v <= LAST2:
                            dve.scalar_tensor_tensor(g_lo[:, gs], norm_view(i), 0.0, f32(g_hi[:, gs]), op0=ALU.max,
                                                     op1=ALU.subtract).then_inc(hs_lo, 1)
                        else:
                            dve.tensor_tensor(h_lo[:, gs], y_view(i), f32(h_hi[:, gs]), ALU.subtract).then_inc(hs_lo, 1)
                    v = due(n, "out", i)
                    if v is not None and v >= HOP2:
                        g = 2 * VISITS[v][1] + i
                        gs = slice(g * BANK, (g + 1) * BANK)
                        dve.wait_ge(y_ok, 2 * (v - LAST2 - 1) + i + 1)
                        dve.tensor_tensor(x[:, gs], y_view(i), x[:, gs], ALU.add).then_inc(o_ok, 1)

        @block.tensor
        def _(pe):
            def product(dst, w_hi, w_lo, m_hi, m_lo, first, last):
                pe.matmul(dst, w_hi, m_hi, start=first, stop=False)
                pe.matmul(dst, w_hi, m_lo, start=False, stop=False)
                return pe.matmul(dst, w_lo, m_hi, start=False, stop=last)

            half = [slice(b * BANK, (b + 1) * BANK) for b in range(2)]

            def tile_product(k, r, first, last, copied, dst=psP, w_hi=h_hi, w_lo=h_lo):
                wh, wl = w_hi[:, k * P:(k + 1) * P], w_lo[:, k * P:(k + 1) * P]
                r_hi, r_lo = hi_at(r), lo_at(r)
                if first or last:
                    for b in range(2):
                        if first and copied is not None:
                            pe.wait_ge(p_out, 2 * copied - 1 + b)
                        end = product(dst[:, b, :], wh, wl, r_hi[:, half[b]], r_lo[:, half[b]], first, last)
                        if last and b == 0:
                            end.then_inc(p_half, 1)
                    return end
                return both_banks(dst, r, wh, wl, False, False)

            def both_banks(dst, r, wh, wl, first, last):
                for m, opens in ((hi_at(r), first), (lo_at(r), False)):
                    for b in range(2):
                        pe.matmul(dst[:, b, :], wh, m[:, half[b]], start=opens, stop=False)
                for b in range(2):
                    end = pe.matmul(dst[:, b, :], wl, hi_at(r)[:, half[b]], start=False, stop=last)
                return end

            def rows(i, t):
                return pt[:, i * BANK + t * P:i * BANK + (t + 1) * P]

            def row_product(bank, src, w):
                for t in range(GT):
                    end = pe.matmul(psE[:, bank, t * P:(t + 1) * P], src(t), w[:, :], start=True, stop=True)
                end.then_inc(e_done, 1)

            pe.wait_ge(ident_ok, 1)

            def q_product(J, q, hj):
                I, u = q // 4, q % 4
                g = J * SLOTS + q
                pe.wait_ge(t_lo, g + 1)
                if u == 0 and not (isinstance(J, int) and J == 0 and I < 2):
                    pe.wait_ge(q_added, J * SUP + I - 1)
                for b in range(2):
                    j = 2 * u + b
                    wh, wl = hj(j)
                    bs = slice(b * BANK, (b + 1) * BANK)
                    end = product(psQ[:, I % 2, :], wh, wl, hi[:, 2 + q % 2, bs], lo[:, 2 + q % 2, bs],
                                  first=(j == 0), last=(j == TS - 1))
                end.then_inc(t_used, 1)

            def transposes(J, q):
                g = J * SLOTS + q
                I, u = q // 4, q % 4
                if u == 0:
                    pe.wait_ge(*nat_landed(J, q))
                    pe.wait_ge(*nat_landed(J, q + 2))
                for b in range(2):
                    if not (isinstance(J, int) and J == 0 and q == 0):
                        pe.wait_ge(t_out, 2 * g + b - 1)
                    j = 2 * u + b
                    for r in range(4):
                        end = pe.transpose(psT[:, b, r * P:(r + 1) * P],
                                           nat_tile(4 * I + r, j * P, P), ident[:, :])
                    end.then_inc(t_done, 1)

            def slab(J, first=False, last=False):
                if first or last:
                    hj = lambda j: (h_hi[:, (J * TS + j) * P:(J * TS + j + 1) * P], h_lo[:, (J * TS + j) * P:(J * TS + j + 1) * P])
                else:
                    hj = lambda j: (hj_hi[:, j * P:(j + 1) * P], hj_lo[:, j * P:(j + 1) * P])
                for q in range(SLOTS + LAG):
                    g = J * SLOTS + q
                    I, u = q // 4, q % 4
                    if q < SLOTS:
                        if q > 0:
                            transposes(J, q)
                        if first and u == 0:
                            pe.wait_ge(hs_lo, I + 1)
                        pe.wait_ge(nat_lo, g + 1)
                        tile_product(q, q % 2, q == 0, q == SLOTS - 1,
                                     None if first else J).then_inc(nat_used, 1)
                    if q == SLOTS + LAG - 1 and not last:
                        transposes(J + 1, 0)
                    if q >= LAG:
                        if q == LAG and not first and not last:
                            pe.wait_ge(hj_hi_ok, J)
                            pe.wait_ge(hj_lo_ok, J)
                        q_product(J, q - LAG, hj)
                    if not first and q in (2, 3):
                        i = q - 2
                        pe.wait_ge(p_out, 2 * J - 1 + i)
                        row_product(i, lambda t, i=i: rows(i, t), wo)
                    if last and u == 3 and 1 <= I < SUP:
                        G = I - 1
                        e = 2 * (SL - 1) + G
                        pe.wait_ge(q_added, J * SUP + G + 1)
                        pe.wait_ge(e_used, e - 1)
                        row_product(G % 2, lambda t, G=G: acc[:, G * BANK + t * P:G * BANK + (t + 1) * P], wi)

            transposes(0, 0)
            slab(0, first=True)
            pe.wait_ge(w_in_sem, 16 * 6)
            with pe.Fori(1, SL - 1) as J:
                slab(J)
            slab(SL - 1, last=True)

            def last_of_pass0(k):
                if k == 2:
                    G = NG - 1
                    pe.wait_ge(q_added, SL * SUP)
                    pe.wait_ge(e_used, 2 * SL + NG - 4)
                    row_product(G % 2, lambda t: acc[:, G * BANK + t * P:G * BANK + (t + 1) * P], wi)
                for i in range(2):
                    if k == 4 + i:
                        pe.wait_ge(p_out, 2 * SL - 1 + i)
                        pe.wait_ge(e_used, 2 * SL + NG - 3 + i)
                        row_product(i, lambda t: rows(i, t), wo)

            def last_chunk(c, k):
                for i in range(2):
                    if k == 4 + i:
                        pe.wait_ge(p_out, 2 * (SL + c) - 1 + i)
                        pe.wait_ge(e_used, E0 + 2 * (c - 1) + i - 1)
                        for t in range(GT):
                            end = pe.transpose(psE[:, i, t * P:(t + 1) * P], rows(i, t), ident[:, :])
                        end.then_inc(e_done, 1)
                    if k == AFTER1["turn"][i]:
                        pe.wait_ge(hn_ok, LN2 + 2 * (c - 1) + i + 1)
                        for t in range(GT):
                            end = pe.transpose(psT[:, i, t * P:(t + 1) * P], rows(i, t), ident[:, :])
                        end.then_inc(ht_done, 1)
                    if k == AFTER1["w_top"][i]:
                        pe.wait_ge(ht_out, 2 * (c - 1) + i + 1)
                        for t in range(GT):
                            end = pe.matmul(psQ[:, i, t * P:(t + 1) * P], stage[:, i, 0, t * P:(t + 1) * P], w2a[:, :],
                                            start=True, stop=True)
                        end.then_inc(g_done, 1)

            def chunk(oc, lead=False, last=False):
                for k in range(T):
                    if lead and k % GT == 0:
                        pe.wait_ge(hs_lo, NG + k // GT + 1)
                    pe.wait_ge(a_lo, oc * T + k + 1)
                    tile_product(k, PLACES1[k], k == 0, k == T - 1, SL + oc).then_inc(a_used, 1)
                    if lead:
                        last_of_pass0(k)
                    else:
                        last_chunk(oc, k)

            chunk(0, lead=True)
            with pe.Fori(1, SL - 1) as oc:
                chunk(oc)
            chunk(SL - 1, last=True)

            for n in range(len(TILES) + TAIL):
                if n < len(TILES):
                    v, k = TILES[n]
                    p, c, Js, both = VISITS[v]
                    first, last = n == END[v] - TS * len(Js), n == END[v] - 1
                    if k % GT == 0:
                        pe.wait_ge(hs_lo, split_count(p, k))
                    pe.wait_ge(a_lo, base(2) + n + 1)
                    if k // TS in both:
                        if k % GT == 0:
                            pe.wait_ge(hs_lo, split_count(p + 1, k))
                        opens = n == END[v] - TS * len(both)
                        if opens and v == BOTH[0]:
                            pe.wait_ge(g_out, 2 * SL)
                        elif opens:
                            pe.wait_ge(part_out, 2 * BOTH.index(v))
                        u_hi, u_lo = (g_hi, g_lo) if p == 2 else (h_hi, h_lo)
                        both_banks(psQ, place2(n), u_hi[:, k * P:(k + 1) * P], u_lo[:, k * P:(k + 1) * P], opens, last)
                    w_hi, w_lo = (g_hi, g_lo) if p == 3 else (h_hi, h_lo)
                    if first and v == 1:
                        pe.wait_ge(ht_out, 2 * SL)
                    tile_product(k, place2(n), first, last, None if v == 1 else chunks_done(max(v - 2, -1)),
                                 product_of(v), w_hi, w_lo).then_inc(a_used, 1)
                if n < T:
                    last_chunk(SL, n)
                for i in range(2):
                    v = due(n, "rows", i)
                    if v is not None:
                        pe.wait_ge(p_out, 2 * chunks_done(v) - 1 + i)
                        pe.wait_ge(e_used, e_index(v, i) - 1)
                        row_product(i, lambda t: rows(i, t), w2b if v <= LAST2 else w3)



_OUTS = [((4096, 128), "float32")]
_INS = ["x", "adj", "L0_gnn_W_in", "L0_gnn_W_out", "L2_gnn_weight", "L3_gnn_W", "L3_gnn_b"]


def kernel(**inputs):
    import numpy as _np
    import concourse.bacc as _bacc
    from concourse import mybir as _mybir
    from concourse.bass_utils import run_bass_kernel_spmd as _run

    nc = _bacc.Bacc("TRN2", target_bir_lowering=False, num_devices=1)
    arrays, args = {}, []
    for name in _INS:
        a = _np.ascontiguousarray(inputs[name])
        arrays[f"in_{name}_dram"] = a
        args.append(nc.dram_tensor(f"in_{name}_dram", a.shape, _mybir.dt.from_np(a.dtype), kind="ExternalInput").ap())
    for i, (shape, dtype) in enumerate(_OUTS):
        dt = _mybir.dt.from_np(_np.dtype(dtype))
        args.append(nc.dram_tensor(f"out_{i}_dram", shape, dt, kind="ExternalOutput").ap())
    gnn_stack_kernel(nc, *args)
    r = _run(nc, [arrays], core_ids=[0])
    return r.results[0]["out_0_dram"]
```
